# Optimizing a Trainium2 kernel written in Bass

```python
import numpy as np
import jax
import jax.numpy as jnp

def _softmax(x, axis=-1):
    return jax.nn.softmax(x, axis=axis)
def _gelu(x):
    return jax.nn.gelu(x, approximate=True)
def _silu(x):
    return jax.nn.silu(x)
def _sigmoid(x):
    return jax.nn.sigmoid(x)
def _layernorm(x, axis=-1, eps=1e-5):
    m = jnp.mean(x, axis=axis, keepdims=True)
    v = jnp.var(x, axis=axis, keepdims=True)
    return (x - m) / jnp.sqrt(v + eps)
def _scatter_add(tgt, idx, src, axis=0):
    return tgt.at[idx].add(src)
def _segment_sum(src, seg, n):
    return jax.ops.segment_sum(src, seg, n)

kernel_name = 'mk_conv_seq_d2_conv_nhwc192_365c93'

def setup_inputs(seed: int = 0):
    np.random.seed(seed)
    _w = jnp.asarray
    def _rec_inputs():
        import jax
        import jax.numpy as jnp
        _gk = jax.random.key(seed)
        x = 0.0002141 + 1 * jax.random.normal(jax.random.fold_in(_gk, 1), (4, 32, 32, 192), jnp.float32)
        return x
    x = _rec_inputs()
    def _L0_conv_setup():
        import jax, jax.numpy as jnp
        from jax import lax
        import numpy as np
        B, H, W, C = (4, 32, 32, 192)
        DEPTH = 9
        DI = int(2.0 * C)
        N = 16
        R = (C + 15) // 16
        K = 4
        MLP_H = int(4.0 * C)

        def layer_norm(x, g, b, eps=1e-05):
            mu = jnp.mean(x, axis=-1, keepdims=True)
            var = jnp.mean(jnp.square(x - mu), axis=-1, keepdims=True)
            return (x - mu) * lax.rsqrt(var + eps) * g + b

        def ssm_scan(u, delta, A, Bs, Cs):
            uL = jnp.moveaxis(u, -1, 0)
            dL = jnp.moveaxis(delta, -1, 0)
            BL = jnp.moveaxis(Bs, -1, 0)
            CL = jnp.moveaxis(Cs, -1, 0)
            h0 = jnp.zeros(u.shape[:3] + (A.shape[-1],), u.dtype)

            def step(h, inp):
                u_t, d_t, B_t, C_t = inp
                h = jnp.exp(d_t[..., None] * A) * h + (d_t * u_t)[..., None] * B_t[:, :, None, :]
                return (h, jnp.einsum('bkdn,bkn->bkd', h, C_t))
            _, ys = lax.scan(step, h0, (uL, dL, BL, CL))
            return jnp.moveaxis(ys, 0, -1)

        def vss_block(x, p):
            n1g, n1b, in_w, conv_w, conv_b, xproj_w, dt_w, dt_b, A_logs, Ds, ong, onb, out_w, n2g, n2b, w1, b1, w2, b2 = p
            b, h, w, _ = x.shape
            L = h * w
            xn = layer_norm(x, n1g, n1b)
            xv, z = jnp.split(xn @ in_w, 2, axis=-1)
            z = jax.nn.silu(z)
            xc = jnp.transpose(xv, (0, 3, 1, 2))
            xc = lax.conv_general_dilated(xc, conv_w, (1, 1), 'SAME', feature_group_count=DI)
            xc = jax.nn.silu(xc + conv_b[None, :, None, None])
            x0 = xc.reshape(b, DI, L)
            x1 = jnp.transpose(xc, (0, 1, 3, 2)).reshape(b, DI, L)
            xs = jnp.stack([x0, x1, x0[:, :, ::-1], x1[:, :, ::-1]], axis=1)
            x_dbl = jnp.einsum('bkdl,kcd->bkcl', xs, xproj_w)
            dts, Bs, Cs = (x_dbl[:, :, :R], x_dbl[:, :, R:R + N], x_dbl[:, :, R + N:])
            delta = jax.nn.softplus(jnp.einsum('bkrl,kdr->bkdl', dts, dt_w) + dt_b[None, :, :, None])
            A = -jnp.exp(A_logs)
            ys = ssm_scan(xs, delta, A, Bs, Cs) + Ds[None, :, :, None] * xs
            y0 = ys[:, 0] + ys[:, 2, :, ::-1]
            y1 = ys[:, 1] + ys[:, 3, :, ::-1]
            y1 = jnp.transpose(y1.reshape(b, DI, w, h), (0, 1, 3, 2)).reshape(b, DI, L)
            y = jnp.transpose((y0 + y1).reshape(b, DI, h, w), (0, 2, 3, 1))
            y = layer_norm(y, ong, onb) * z
            x = x + y @ out_w
            h2 = jax.nn.gelu(layer_norm(x, n2g, n2b) @ w1 + b1, approximate=False)
            return x + (h2 @ w2 + b2)
        key = jax.random.key(seed)
        ks = iter(jax.random.split(key, 32))

        def rn(shape, s=0.02):
            return jax.random.normal(next(ks), shape, jnp.float32) * s
        return dict(x=jax.random.normal(next(ks), (B, H, W, C), jnp.float32), n1g=jnp.ones((DEPTH, C)), n1b=jnp.zeros((DEPTH, C)), in_w=rn((DEPTH, C, 2 * DI)), conv_w=rn((DEPTH, DI, 1, 3, 3), 0.1), conv_b=jnp.zeros((DEPTH, DI)), xproj_w=rn((DEPTH, K, R + 2 * N, DI)), dt_w=rn((DEPTH, K, DI, R), 0.1), dt_b=rn((DEPTH, K, DI), 0.5), A_logs=jnp.log(jax.random.uniform(next(ks), (DEPTH, K, DI, N), jnp.float32, 0.5, 8.0)), Ds=jnp.ones((DEPTH, K, DI)), ong=jnp.ones((DEPTH, DI)), onb=jnp.zeros((DEPTH, DI)), out_w=rn((DEPTH, DI, C)), n2g=jnp.ones((DEPTH, C)), n2b=jnp.zeros((DEPTH, C)), w1=rn((DEPTH, C, MLP_H)), b1=jnp.zeros((DEPTH, MLP_H)), w2=rn((DEPTH, MLP_H, C)), b2=jnp.zeros((DEPTH, C)))
    _L0_conv_all = _L0_conv_setup()
    _L0_conv_in = {k: v for k, v in _L0_conv_all.items() if k in ('n1g', 'n1b', 'in_w', 'conv_w', 'conv_b', 'xproj_w', 'dt_w', 'dt_b', 'A_logs', 'Ds', 'ong', 'onb', 'out_w', 'n2g', 'n2b', 'w1', 'b1', 'w2', 'b2', )}
    del _L0_conv_all

    def _L1_conv_setup():
        import jax, jax.numpy as jnp
        import numpy as np
        B_SZ, H_DIM, W_DIM, D_MODEL = (2, 64, 64, 192)
        N_STATE = 16
        R_RANK = 12
        K_DIRS = 4
        LN_EPS = 1e-05

        def _cross_scan(x):
            b, d, h, w = x.shape
            x0 = x.reshape(b, d, h * w)
            x1 = jnp.transpose(x, (0, 1, 3, 2)).reshape(b, d, h * w)
            xs = jnp.stack([x0, x1], axis=1)
            return jnp.concatenate([xs, jnp.flip(xs, axis=-1)], axis=1)

        def _cross_merge(ys, h, w):
            b, _, d, l = ys.shape
            ys = ys[:, 0:2] + jnp.flip(ys[:, 2:4], axis=-1)
            y1 = jnp.transpose(ys[:, 1].reshape(b, d, w, h), (0, 1, 3, 2)).reshape(b, d, l)
            return ys[:, 0] + y1

        def _selective_scan(xs, dts, A, Bs, Cs):
            b, k, d, l = xs.shape
            n = A.shape[-1]

            @jax.checkpoint
            def step(h_prev, t):
                x_t, dt_t, B_t, C_t = t
                dA = jnp.exp(dt_t[..., None] * A)
                dBx = (dt_t * x_t)[..., None] * B_t[:, :, None, :]
                h = dA * h_prev + dBx
                y = jnp.einsum('bkdn,bkn->bkd', h, C_t)
                return (h, y)
            seq = (jnp.moveaxis(xs, -1, 0), jnp.moveaxis(dts, -1, 0), jnp.moveaxis(Bs, -1, 0), jnp.moveaxis(Cs, -1, 0))
            h0 = jnp.zeros((b, k, d, n), xs.dtype)
            _, ys = jax.lax.scan(step, h0, seq)
            return jnp.moveaxis(ys, 0, -1)
        key = jax.random.key(seed)
        ks = jax.random.split(key, 5)
        x = jax.random.normal(ks[0], (B_SZ, H_DIM, W_DIM, D_MODEL), jnp.float32)
        x_proj_weight = jax.random.normal(ks[1], (K_DIRS, R_RANK + 2 * N_STATE, D_MODEL), jnp.float32) * 0.02
        dt_projs_weight = jax.random.uniform(ks[2], (K_DIRS, D_MODEL, R_RANK), jnp.float32, -R_RANK ** (-0.5), R_RANK ** (-0.5))
        dt = jnp.exp(jax.random.uniform(ks[3], (K_DIRS, D_MODEL)) * (np.log(0.1) - np.log(0.001)) + np.log(0.001))
        dt = jnp.clip(dt, 0.0001, None)
        dt_projs_bias = dt + jnp.log(-jnp.expm1(-dt))
        A_logs = jnp.log(jnp.tile(jnp.arange(1, N_STATE + 1, dtype=jnp.float32), (K_DIRS * D_MODEL, 1)))
        Ds = jnp.ones((K_DIRS * D_MODEL,), jnp.float32)
        ln_weight = jnp.ones((D_MODEL,), jnp.float32)
        ln_bias = jnp.zeros((D_MODEL,), jnp.float32)
        return dict(x=x, x_proj_weight=x_proj_weight, dt_projs_weight=dt_projs_weight, dt_projs_bias=dt_projs_bias, A_logs=A_logs, Ds=Ds, ln_weight=ln_weight, ln_bias=ln_bias)
    _L1_conv_all = _L1_conv_setup()
    _L1_conv_in = {k: v for k, v in _L1_conv_all.items() if k in ('x_proj_weight', 'dt_projs_weight', 'dt_projs_bias', 'A_logs', 'Ds', 'ln_weight', 'ln_bias', )}
    del _L1_conv_all

    return {
        "x": x,
        "L0_conv_n1g": _L0_conv_in["n1g"],
        "L0_conv_n1b": _L0_conv_in["n1b"],
        "L0_conv_in_w": _L0_conv_in["in_w"],
        "L0_conv_conv_w": _L0_conv_in["conv_w"],
        "L0_conv_conv_b": _L0_conv_in["conv_b"],
        "L0_conv_xproj_w": _L0_conv_in["xproj_w"],
        "L0_conv_dt_w": _L0_conv_in["dt_w"],
        "L0_conv_dt_b": _L0_conv_in["dt_b"],
        "L0_conv_A_logs": _L0_conv_in["A_logs"],
        "L0_conv_Ds": _L0_conv_in["Ds"],
        "L0_conv_ong": _L0_conv_in["ong"],
        "L0_conv_onb": _L0_conv_in["onb"],
        "L0_conv_out_w": _L0_conv_in["out_w"],
        "L0_conv_n2g": _L0_conv_in["n2g"],
        "L0_conv_n2b": _L0_conv_in["n2b"],
        "L0_conv_w1": _L0_conv_in["w1"],
        "L0_conv_b1": _L0_conv_in["b1"],
        "L0_conv_w2": _L0_conv_in["w2"],
        "L0_conv_b2": _L0_conv_in["b2"],
        "L1_conv_x_proj_weight": _L1_conv_in["x_proj_weight"],
        "L1_conv_dt_projs_weight": _L1_conv_in["dt_projs_weight"],
        "L1_conv_dt_projs_bias": _L1_conv_in["dt_projs_bias"],
        "L1_conv_A_logs": _L1_conv_in["A_logs"],
        "L1_conv_Ds": _L1_conv_in["Ds"],
        "L1_conv_ln_weight": _L1_conv_in["ln_weight"],
        "L1_conv_ln_bias": _L1_conv_in["ln_bias"],
    }

def reference(x, L0_conv_n1g, L0_conv_n1b, L0_conv_in_w, L0_conv_conv_w, L0_conv_conv_b, L0_conv_xproj_w, L0_conv_dt_w, L0_conv_dt_b, L0_conv_A_logs, L0_conv_Ds, L0_conv_ong, L0_conv_onb, L0_conv_out_w, L0_conv_n2g, L0_conv_n2b, L0_conv_w1, L0_conv_b1, L0_conv_w2, L0_conv_b2, L1_conv_x_proj_weight, L1_conv_dt_projs_weight, L1_conv_dt_projs_bias, L1_conv_A_logs, L1_conv_Ds, L1_conv_ln_weight, L1_conv_ln_bias):
    import jax
    import jax.numpy as jnp
    def _L0_conv_ref(x, n1g, n1b, in_w, conv_w, conv_b, xproj_w, dt_w, dt_b, A_logs, Ds, ong, onb, out_w, n2g, n2b, w1, b1, w2, b2):
        import jax, jax.numpy as jnp
        from jax import lax
        import numpy as np
        B, H, W, C = (4, 32, 32, 192)
        DEPTH = 9
        DI = int(2.0 * C)
        N = 16
        R = (C + 15) // 16
        K = 4
        MLP_H = int(4.0 * C)

        def layer_norm(x, g, b, eps=1e-05):
            mu = jnp.mean(x, axis=-1, keepdims=True)
            var = jnp.mean(jnp.square(x - mu), axis=-1, keepdims=True)
            return (x - mu) * lax.rsqrt(var + eps) * g + b

        def ssm_scan(u, delta, A, Bs, Cs):
            uL = jnp.moveaxis(u, -1, 0)
            dL = jnp.moveaxis(delta, -1, 0)
            BL = jnp.moveaxis(Bs, -1, 0)
            CL = jnp.moveaxis(Cs, -1, 0)
            h0 = jnp.zeros(u.shape[:3] + (A.shape[-1],), u.dtype)

            def step(h, inp):
                u_t, d_t, B_t, C_t = inp
                h = jnp.exp(d_t[..., None] * A) * h + (d_t * u_t)[..., None] * B_t[:, :, None, :]
                return (h, jnp.einsum('bkdn,bkn->bkd', h, C_t))
            _, ys = lax.scan(step, h0, (uL, dL, BL, CL))
            return jnp.moveaxis(ys, 0, -1)

        def vss_block(x, p):
            n1g, n1b, in_w, conv_w, conv_b, xproj_w, dt_w, dt_b, A_logs, Ds, ong, onb, out_w, n2g, n2b, w1, b1, w2, b2 = p
            b, h, w, _ = x.shape
            L = h * w
            xn = layer_norm(x, n1g, n1b)
            xv, z = jnp.split(xn @ in_w, 2, axis=-1)
            z = jax.nn.silu(z)
            xc = jnp.transpose(xv, (0, 3, 1, 2))
            xc = lax.conv_general_dilated(xc, conv_w, (1, 1), 'SAME', feature_group_count=DI)
            xc = jax.nn.silu(xc + conv_b[None, :, None, None])
            x0 = xc.reshape(b, DI, L)
            x1 = jnp.transpose(xc, (0, 1, 3, 2)).reshape(b, DI, L)
            xs = jnp.stack([x0, x1, x0[:, :, ::-1], x1[:, :, ::-1]], axis=1)
            x_dbl = jnp.einsum('bkdl,kcd->bkcl', xs, xproj_w)
            dts, Bs, Cs = (x_dbl[:, :, :R], x_dbl[:, :, R:R + N], x_dbl[:, :, R + N:])
            delta = jax.nn.softplus(jnp.einsum('bkrl,kdr->bkdl', dts, dt_w) + dt_b[None, :, :, None])
            A = -jnp.exp(A_logs)
            ys = ssm_scan(xs, delta, A, Bs, Cs) + Ds[None, :, :, None] * xs
            y0 = ys[:, 0] + ys[:, 2, :, ::-1]
            y1 = ys[:, 1] + ys[:, 3, :, ::-1]
            y1 = jnp.transpose(y1.reshape(b, DI, w, h), (0, 1, 3, 2)).reshape(b, DI, L)
            y = jnp.transpose((y0 + y1).reshape(b, DI, h, w), (0, 2, 3, 1))
            y = layer_norm(y, ong, onb) * z
            x = x + y @ out_w
            h2 = jax.nn.gelu(layer_norm(x, n2g, n2b) @ w1 + b1, approximate=False)
            return x + (h2 @ w2 + b2)
        params = (n1g, n1b, in_w, conv_w, conv_b, xproj_w, dt_w, dt_b, A_logs, Ds, ong, onb, out_w, n2g, n2b, w1, b1, w2, b2)
        for i in range(DEPTH):
            x = vss_block(x, tuple((a[i] for a in params)))
        return x

    def _L1_conv_ref(x, x_proj_weight, dt_projs_weight, dt_projs_bias, A_logs, Ds, ln_weight, ln_bias):
        import jax, jax.numpy as jnp
        import numpy as np
        B_SZ, H_DIM, W_DIM, D_MODEL = (2, 64, 64, 192)
        N_STATE = 16
        R_RANK = 12
        K_DIRS = 4
        LN_EPS = 1e-05

        def _cross_scan(x):
            b, d, h, w = x.shape
            x0 = x.reshape(b, d, h * w)
            x1 = jnp.transpose(x, (0, 1, 3, 2)).reshape(b, d, h * w)
            xs = jnp.stack([x0, x1], axis=1)
            return jnp.concatenate([xs, jnp.flip(xs, axis=-1)], axis=1)

        def _cross_merge(ys, h, w):
            b, _, d, l = ys.shape
            ys = ys[:, 0:2] + jnp.flip(ys[:, 2:4], axis=-1)
            y1 = jnp.transpose(ys[:, 1].reshape(b, d, w, h), (0, 1, 3, 2)).reshape(b, d, l)
            return ys[:, 0] + y1

        def _selective_scan(xs, dts, A, Bs, Cs):
            b, k, d, l = xs.shape
            n = A.shape[-1]

            @jax.checkpoint
            def step(h_prev, t):
                x_t, dt_t, B_t, C_t = t
                dA = jnp.exp(dt_t[..., None] * A)
                dBx = (dt_t * x_t)[..., None] * B_t[:, :, None, :]
                h = dA * h_prev + dBx
                y = jnp.einsum('bkdn,bkn->bkd', h, C_t)
                return (h, y)
            seq = (jnp.moveaxis(xs, -1, 0), jnp.moveaxis(dts, -1, 0), jnp.moveaxis(Bs, -1, 0), jnp.moveaxis(Cs, -1, 0))
            h0 = jnp.zeros((b, k, d, n), xs.dtype)
            _, ys = jax.lax.scan(step, h0, seq)
            return jnp.moveaxis(ys, 0, -1)
        b, h, w, d = x.shape
        l = h * w
        xc = jnp.transpose(x, (0, 3, 1, 2))
        xs = _cross_scan(xc)
        x_dbl = jnp.einsum('bkdl,kcd->bkcl', xs, x_proj_weight)
        dts, Bs, Cs = jnp.split(x_dbl, [R_RANK, R_RANK + N_STATE], axis=2)
        dts = jnp.einsum('bkrl,kdr->bkdl', dts, dt_projs_weight)
        dts = jax.nn.softplus(dts + dt_projs_bias[None, :, :, None])
        A = -jnp.exp(A_logs).reshape(K_DIRS, d, N_STATE)
        ys = _selective_scan(xs, dts, A, Bs, Cs)
        ys = ys + Ds.reshape(1, K_DIRS, d, 1) * xs
        y = _cross_merge(ys, h, w)
        y = jnp.transpose(y, (0, 2, 1))
        mu = jnp.mean(y, -1, keepdims=True)
        var = jnp.mean(jnp.square(y - mu), -1, keepdims=True)
        y = (y - mu) * jax.lax.rsqrt(var + LN_EPS) * ln_weight + ln_bias
        return y.reshape(b, h, w, d)

    def _gn(v, G=32, eps=1e-5):
        B_, H_, W_, C_ = v.shape
        g = v.reshape(B_, H_, W_, G, C_ // G)
        m = jnp.mean(g, axis=(1, 2, 4), keepdims=True)
        s = jnp.var(g, axis=(1, 2, 4), keepdims=True)
        return ((g - m) / jnp.sqrt(s + eps)).reshape(v.shape)

    def _ln_c(v, eps=1e-6):
        m = jnp.mean(v, axis=-1, keepdims=True)
        s = jnp.var(v, axis=-1, keepdims=True)
        return (v - m) / jnp.sqrt(s + eps)

    def _ln_t(v, eps=1e-5):
        m = jnp.mean(v, axis=-1, keepdims=True)
        s = jnp.var(v, axis=-1, keepdims=True)
        return (v - m) / jnp.sqrt(s + eps)

    def _to_tokens(v):
        B_, H_, W_, C_ = v.shape
        return v.reshape(B_, H_ * W_, C_)
    def _from_tokens(t, like):
        return t.reshape(like.shape)

    x = _L0_conv_ref(x, L0_conv_n1g, L0_conv_n1b, L0_conv_in_w, L0_conv_conv_w, L0_conv_conv_b, L0_conv_xproj_w, L0_conv_dt_w, L0_conv_dt_b, L0_conv_A_logs, L0_conv_Ds, L0_conv_ong, L0_conv_onb, L0_conv_out_w, L0_conv_n2g, L0_conv_n2b, L0_conv_w1, L0_conv_b1, L0_conv_w2, L0_conv_b2)
    x = _L1_conv_ref(x, L1_conv_x_proj_weight, L1_conv_dt_projs_weight, L1_conv_dt_projs_bias, L1_conv_A_logs, L1_conv_Ds, L1_conv_ln_weight, L1_conv_ln_bias)
    return x


_drawn_inputs = setup_inputs


def setup_inputs(seed=0):
    import zlib

    import numpy as np

    out = dict(_drawn_inputs(seed))
    spreads = {'L0_conv_n1g': (1.0, 0.2),
     'L0_conv_n1b': (0.0, 0.412),
     'L0_conv_conv_b': (0.0, 0.1),
     'L0_conv_Ds': (1.0, 0.6),
     'L0_conv_ong': (1.0, 0.2),
     'L0_conv_onb': (0.0, 0.489),
     'L0_conv_n2g': (1.0, 0.2),
     'L0_conv_n2b': (0.0, 0.358),
     'L0_conv_b1': (0.0, 0.1),
     'L0_conv_b2': (0.0, 0.1),
     'L1_conv_Ds': (1.0, 0.2),
     'L1_conv_ln_weight': (1.0, 0.2),
     'L1_conv_ln_bias': (0.0, 0.1)}
    factors = {'L0_conv_xproj_w': 8.0,
     'L0_conv_dt_w': 8.0,
     'L0_conv_dt_b': 8.0,
     'L0_conv_A_logs': 8.0,
     'L1_conv_x_proj_weight': 5.294,
     'L1_conv_dt_projs_weight': 8.0,
     'L1_conv_dt_projs_bias': 8.0,
     'L1_conv_A_logs': 8.0}
    for name, (base, spread) in spreads.items():
        noise = np.random.default_rng([zlib.crc32(name.encode()), seed]).standard_normal(out[name].shape)
        drawn = base * np.exp(spread * noise) if base else spread * noise
        out[name] = jnp.asarray(drawn.astype(out[name].dtype))
    for name, factor in factors.items():
        out[name] = (out[name] * factor).astype(out[name].dtype)
    return out
```

```python
import concourse.bass as bass
from concourse import mybir
from contextlib import ExitStack

BATCH, HH, WW, C = 4, 32, 32, 192
L = HH * WW
DEPTH, DI, NS, R, K, MLP = 9, 384, 16, 12, 4, 768
HALF = 512
TOK = L // 128
PC, CT = 96, 2
NB = 8
NH = NS // NB
EARLY = NB + 1
MT = MLP // 128
SLOTS = 4
DELTA_AT = (0, 1, 3, NB - 1)
XR = 2 * NS + R
LN_EPS = 1e-5

V_CW, V_CB, V_DTB, V_AL, V_DS, V_OG, V_OB, V_B1, V_END = 0, 27, 30, 42, 234, 246, 249, 252, 258
U_DTB, U_AL, U_DS, U_END = 0, 8, 136, 144


class Count:

    def __init__(self, sem, first, per0, per1):
        self.sem, self.first, self.per0, self.per1 = sem, first, per0, per1


def build(nc, x, w_in, w_xp, w_dt, w_out, w_1, w_2, vec, vec96, b2, l_xp, l_dt, l_vec, l_ln, out):
    f32, bf16 = mybir.dt.float32, mybir.dt.bfloat16
    ALU = mybir.AluOpType
    ACT = mybir.ActivationFunctionType
    AX = mybir.AxisListType.X

    ctx = ExitStack()
    with ctx:
        def sb(name, shape, dt=f32):
            return ctx.enter_context(nc.sbuf_tensor(name, shape, dt))

        x_dram = nc.dram_tensor("x_between", (BATCH, L, C), f32, kind="Internal").ap()
        z_dram = nc.dram_tensor("z_parked", (128, 3 * L), f32, kind="Internal").ap()

        bc = sb("bc", [128, 2, NB, L])
        delta = sb("delta", [128, 3, L])
        du = sb("du", [128, 3, L])
        db = sb("db", [128, SLOTS, L])
        hc = sb("hc", [128, SLOTS, L])
        sp_e = sb("sp_e", [128, L])
        sp_s = sb("sp_s", [128, L])
        sp_l = sb("sp_l", [128, L])
        xc = sb("xc", [128, 3, L])
        ysb = sb("ysb", [128, 3, L])
        bcr = sb("bcr", [64, L])
        dts = sb("dts", [R, L])
        split = sb("split", [96, L], bf16)
        sel = sb("sel", [96, 32], bf16)
        ident = sb("ident", [128, 128])
        ones = sb("ones", [1, 128])
        A = sb("A", [128, 3 * K * NS])
        ds_sum = sb("ds_sum", [128, 3])
        eps = sb("eps", [128, 1])
        one = sb("one", [128, 1])
        ln_one = sb("ln_one", [128, 1])
        win = sb("win", [PC, CT, 2 * DI])
        wxp = sb("wxp", [128, 3, K, XR])
        wdt = sb("wdt", [R, K, DI])
        wout = sb("wout", [128, 3, C])
        w1 = sb("w1", [PC, CT, MLP])
        w2 = sb("w2", [128, MT, C])
        vc = sb("vc", [128, V_END])
        vc96 = sb("vc96", [PC, 8])
        b2r = sb("b2r", [1, C])
        lnw = sb("lnw", [128, 2 * C])
        st6 = sb("st6", [128, TOK, 6])
        mv = sb("mv", [128, TOK, 2])
        sd = sb("sd", [128, TOK])
        rstd = sb("rstd", [128, TOK])

        flat = bc[:, :, :, :].rearrange("p a n l -> p (a n l)")
        o = 0

        def part(n, p=128):
            nonlocal o
            o += n
            return flat[0:p, o - n:o]
        xt = part(TOK * C).rearrange("p (j c) -> p j c", j=TOK)
        xn = part(TOK * C).rearrange("p (j c) -> p j c", j=TOK)
        xnT = part(CT * L, PC).rearrange("p (c t) -> p c t", c=CT)
        zb = part(3 * L).rearrange("p (c t) -> p c t", c=3)
        gt = part(3 * L).rearrange("p (c t) -> p c t", c=3)
        yn = part(TOK * DI).rearrange("p (j c) -> p j c", j=TOK)
        PAD = (HH + 2) * (WW + 2)
        xpad = flat[:, o - TOK * DI - 3 * L:o - TOK * DI - 3 * L + 3 * PAD].rearrange(
            "p (c h w) -> p c h w", c=3, h=HH + 2)
        hid = flat[:, o - TOK * DI - 3 * L:o - TOK * DI - 3 * L + MT * L].rearrange("p (m t) -> p m t", m=MT)
        assert o <= 2 * NB * L

        ps = ctx.enter_context(nc.psum_tensor("ps", [128, 8, HALF], f32))

        def bank2(b, p=128):
            return ps[0:p, b:b + 2, :].rearrange("p a b -> p (a b)")
        Y, ST = 4, 6


        def count(name, first=0, per0=0, per1=0):
            return Count(ctx.enter_context(nc.semaphore(name)), first, per0, per1)

        S0, S1 = K * NS * 3, K * NS * CT
        G0, G1 = K * NH * 3, K * NH * CT
        consts = count("consts")
        w_loaded = count("w_loaded")
        w_made = count("w_made")
        gate_pe = count("gate_pe")
        gate_dve = count("gate_dve")
        gate_sp = count("gate_sp")
        gate_pool = count("gate_pool")
        ds_made = count("ds_made")
        x_loaded = count("x_loaded", 0, 32, 16)
        stats = count("stats", 0, 24, 8)
        stats6 = count("stats6", 0, 24, 8)
        sd_done = count("sd_done", 0, 3, 1)
        rstd_done = count("rstd_done", 0, 3, 1)
        normed = count("normed", 0, 3, 1)
        turned = count("turned", 0, 4, 2)
        turned_out = count("turned_out", 0, 2, 0)
        pad_zero = count("pad_zero", 0, 1, 0)
        in_proj = count("in_proj", 0, 6, 0)
        in_evac = count("in_evac", 0, 6, 0)
        conv_step = count("conv_step", 0, 27, 0)
        xc_ready = count("xc_ready", 0, 1, 1)
        z_stored = count("z_stored", 0, 16, 0)
        z_loaded = count("z_loaded", 0, 16, 0)
        st_full = count("st_full", 0, K * (1 + 3 + 2 * NS), K * (1 + CT + 2 * NS))
        st_free = count("st_free", 0, K * (1 + 3), K * (1 + CT))
        hi_done = count("hi_done", 0, K, K)
        r1_done = count("r1_done", 0, K, K)
        mid_done = count("mid_done", 0, K, K)
        lo_done = count("lo_done", 1, K, K)
        abs_done = count("abs_done", 0, K * 3, K * CT)
        e_done = count("e_done", 0, K * 3, K * CT)
        s_done = count("s_done", 0, K * 3, K * CT)
        ln_done = count("ln_done", 0, K * 3, K * CT)
        rem_done = count("rem_done", 0, K * 3, K * CT)
        sum_done = count("sum_done", 0, K * 3, K * CT)
        delta_done = count("delta_done", 1, K * 3, K * CT)
        du_done = count("du_done", 0, K * 3, K * CT)
        bc_ready = count("bc_ready", 0, K * 2 * NS, K * 2 * NS)
        exp_done = count("exp_done", 0, S0, S1)
        mul1_done = count("mul1_done", 2, S0, S1)
        scan_done = count("scan_done", SLOTS, S0, S1)
        mul2_done = count("mul2_done", 2, S0, S1)
        summed = count("summed", SLOTS, S0, S1)
        y_evac = count("y_evac", 1, G0 - 3, G1 - CT)
        y_final = count("y_final", 1, 3, CT)
        yT_out = count("yT_out", 0, 1, 0)
        scaled = count("scaled", 0, 3, 0)
        gated = count("gated", 0, 1, 0)
        out_proj = count("out_proj", 0, 1, 0)
        x_mid = count("x_mid", 0, 1, 0)
        up_proj = count("up_proj", 0, MT, 0)
        gelu_done = count("gelu_done", 0, MT, 0)
        down_proj = count("down_proj", 0, 1, 0)
        x_new = count("x_new", 0, 1, 2)
        x_stored = count("x_stored", 16, 16, 16)
        NW0, NW1 = 9, 4

        class Image:

            def __init__(self, closing, it):
                self.closing, self.it = closing, it
                self.P, self.T = (PC, CT) if closing else (128, 3)
                self.unit, self.free = UNITS[self.T]
                self.dtb = U_DTB if closing else V_DTB

            def at(self, c, k):
                if self.closing:
                    return self.it * c.per1 + (c.first + DEPTH * BATCH * c.per0 + k)
                return self.it * c.per0 + (c.first + k)

        def side_work(T, s):
            g, n = s // NB, s % NB
            k, nh, tile = g // (NH * T), g // T % NH, g % T
            nk, nn = (k, 1) if nh == 0 else (k + 1, 0)
            found = []
            if tile == 0:
                at_n = {1: (0,), 2: (1,), 3: (2, 3), 4: (4, 5), 5: (6,)}.get(n, ())
                found += [("spread", k, nh, EARLY + i) for i in at_n]
            if nh == 0 and tile + 1 < T and n in DELTA_AT:
                found.append(("delta", k, tile + 1, DELTA_AT.index(n)))
            if nh == 1 and k + 1 < K:
                if T == 3 and tile == 1 and n % 2 == 0:
                    found.append(("rows", k + 1, n // 2))
                if T == 2 and tile == 0 and n >= NB - 2:
                    found += [("rows", k + 1, 2 * (n - NB + 2)), ("rows", k + 1, 2 * (n - NB + 2) + 1)]
                if tile == T - 1 and n in DELTA_AT:
                    found.append(("delta", k + 1, 0, DELTA_AT.index(n)))
            if tile == T - 1 and nk < K:
                found += [("spread", nk, nn, n)] + [("spread", nk, nn, EARLY - 1)] * (n == NB - 1)
            return found

        def scans(T, rows, delta_of, spread, step, evac, ahead=0):
            do = {"rows": rows, "delta": delta_of, "spread": spread}
            for stage in range(4):
                rows(0, stage)
            for stage in range(4):
                delta_of(0, 0, stage)
            for i in range(EARLY):
                spread(0, 0, i)
            steps = K * NS * T
            for s in range(ahead):
                for what, *args in side_work(T, s):
                    do[what](*args)
            for s in range(steps):
                g, n = s // NB, s % NB
                if ahead and s + ahead < steps:
                    for what, *args in side_work(T, s + ahead):
                        do[what](*args)
                step(g, g // (NH * T), g // T % NH, g % T, n)
                if not ahead:
                    for what, *args in side_work(T, s):
                        do[what](*args)
                if n == 1 and g:
                    h = g - 1
                    evac(h, h // (NH * T), h // T % NH, h % T)
            evac(g, K - 1, NH - 1, T - 1)

        def count_units(T):
            number, free, counts = {}, {}, {st_free: 0, bc_ready: 0}

            def unit(name, reader):
                if number:
                    free[name] = (before[0], counts[before[0]])
                number[name] = len(number)
                before[0] = reader
                counts[reader] += 1

            before = [None]
            scans(T, lambda k, stage: stage or unit(("rows", k), st_free),
                  lambda k, tile, stage: stage or unit(("delta", k, tile), st_free),
                  lambda k, nh, i: unit(("spread", k, nh, i), bc_ready), lambda *a: None, lambda *a: None)
            return number, free

        UNITS = {3: count_units(3), CT: count_units(CT)}

        def images(e, layer_start, image):
            with e.Fori(0, DEPTH) as l:
                layer_start(l)
                with e.Fori(0, BATCH) as b:
                    image(Image(False, l * BATCH + b), b)
            layer_start(None)
            with e.Fori(0, BATCH) as b:
                image(Image(True, b), b)

        def weights_there(e, l):
            e.wait_ge(w_loaded.sem, 16 * NW0 * DEPTH + 16 * NW1 if l is None else l * (16 * NW0) + 16 * NW0)

        def in_time(ap, k):
            return ap.rearrange("p (h w) -> p w h", h=HH) if k % 2 else ap.rearrange("p (h w) -> p h w", h=HH)

        def idle(*_):
            pass

        def rows_of(ap):
            return ap.rearrange("p (a b) -> p a b", a=32)

        def backward(ap, k):
            return ap[:, ::-1] if k >= 2 else ap

        def y_taken(I, g):
            n_act = (K * NH - 1) * I.T
            return (y_final, 0) if g == 0 else (y_evac, g) if g <= n_act else (y_final, g - n_act)

        block = ctx.enter_context(nc.Block())

        @block.sync
        def _(e):
            e.dma_start(x_dram.rearrange("b t c -> (b t) c"), x.rearrange("b h w c -> (b h w) c"))\
                .then_inc(x_stored.sem, 16)

            def layer_start(l):
                if l is None:
                    e.wait_ge(x_stored.sem, 16 + 16 * DEPTH * BATCH)
                    e.sem_inc(gate_sp.sem, 1)
                    for dst, src in ((wxp[0:PC, 0:CT, :, :].rearrange("p a b c -> p (a b c)"), l_xp),
                                     (wdt[:, :, 0:C], l_dt.rearrange("r (k d) -> r k d", k=K)),
                                     (vc[0:PC, 0:U_END], l_vec),
                                     (lnw[:, :], l_ln.broadcast_to((128, 2 * C)))):
                        e.dma_start(dst, src).then_inc(w_loaded.sem, 16)
                    return
                e.wait_ge(x_stored.sem, l * (16 * BATCH) + 16)
                e.sem_inc(gate_sp.sem, 1)
                for dst, src in ((win[:, :, :].rearrange("p a b -> p (a b)"), w_in),
                                 (wxp[:, :, :, :].rearrange("p a b c -> p (a b c)"), w_xp),
                                 (wdt[:, :, :].rearrange("p a b -> p (a b)"), w_dt),
                                 (wout[:, :, :].rearrange("p a b -> p (a b)"), w_out),
                                 (w1[:, :, :].rearrange("p a b -> p (a b)"), w_1),
                                 (w2[:, :, :].rearrange("p a b -> p (a b)"), w_2),
                                 (vc[:, :], vec), (vc96[:, :], vec96), (b2r[:, :], b2)):
                    e.dma_start(dst, src[bass.ds(l, 1), :, :].rearrange("o p n -> (o p) n"))\
                        .then_inc(w_loaded.sem, 16)

            def image(I, b):
                x_img = x_dram[bass.ds(b, 1), :, :].rearrange("o (j p) c -> p (o j) c", p=128)
                e.wait_ge(x_stored.sem, I.at(x_stored, 0))
                e.sem_inc(gate_sp.sem, 1)
                e.dma_start(xt, x_img).then_inc(x_loaded.sem, 16)
                if I.closing:
                    e.wait_ge(x_new.sem, I.at(x_new, 2))
                    e.sem_inc(gate_sp.sem, 1)
                    e.dma_start(out[bass.ds(b, 1), :, :, :].rearrange("o h w c -> (o h w) c")
                                .rearrange("(j p) c -> p j c", p=128), xn).then_inc(x_stored.sem, 16)
                    return
                e.wait_ge(in_evac.sem, I.at(in_evac, 6))
                e.sem_inc(gate_sp.sem, 1)
                e.dma_start(z_dram.rearrange("p (c t) -> p c t", c=3), zb).then_inc(z_stored.sem, 16)
                e.wait_ge(z_stored.sem, I.at(z_stored, 16))
                e.sem_inc(gate_sp.sem, 1)
                e.wait_ge(summed.sem, I.at(summed, S0))
                e.sem_inc(gate_sp.sem, 1)
                e.wait_ge(mul1_done.sem, I.at(mul1_done, S0))
                e.sem_inc(gate_sp.sem, 1)
                e.dma_start(xt, x_img).then_inc(x_loaded.sem, 16)
                e.dma_start(zb, z_dram.rearrange("p (c t) -> p c t", c=3)).then_inc(z_loaded.sem, 16)
                e.wait_ge(x_new.sem, I.at(x_new, 1))
                e.sem_inc(gate_sp.sem, 1)
                e.dma_start(x_img, xt).then_inc(x_stored.sem, 16)

            images(e, layer_start, image)
            e.wait_ge(x_stored.sem, 16 + 16 * DEPTH * BATCH + 16 * BATCH)

        @block.gpsimd
        def _(e):
            e.sem_inc(mul1_done.sem, 2)
            e.sem_inc(delta_done.sem, 1)
            e.memset(ident[:, :], 0.0).then_inc(consts.sem, 1)
            e.memset(sel[:, :], 0.0).then_inc(consts.sem, 1)
            e.memset(ones[:, :], 1.0).then_inc(consts.sem, 1)
            e.memset(eps[:, :], LN_EPS).then_inc(consts.sem, 1)
            e.memset(one[:, :], 1.0).then_inc(consts.sem, 1)
            e.wait_ge(consts.sem, 2)
            e.affine_select(out=ident[:, :], in_=ident[:, :], compare_op=ALU.not_equal, fill=1.0, base=0,
                            pattern=[[-1, 128]], channel_multiplier=1).then_inc(consts.sem, 1)
            for third in range(3):
                e.wait_ge(consts.sem, 6 + third)
                e.affine_select(out=sel[:, :], in_=sel[:, :], compare_op=ALU.not_equal, fill=1.0,
                                base=-32 * third, pattern=[[-1, 32]], channel_multiplier=1)\
                    .then_inc(consts.sem, 1)

            def image(I, b):
                P, T = I.P, I.T
                if not I.closing:
                    e.wait_ge(x_stored.sem, I.at(x_stored, 0))
                    e.sem_inc(gate_pool.sem, 1)
                    e.memset(xpad, 0.0).then_inc(pad_zero.sem, 1)

                def delta_of(k, tile, stage):
                    i, d = k * T + tile, delta[0:P, tile, :]
                    if stage == 3:
                        e.wait_ge(rem_done.sem, I.at(rem_done, i + 1))
                        e.wait_ge(sum_done.sem, I.at(sum_done, i + 1))
                        e.tensor_tensor(out=d, in0=sp_l[0:P, :], in1=sp_e[0:P, :], op=ALU.subtract)\
                            .then_inc(delta_done.sem, 1)
                        if i == 0:
                            e.wait_ge(xc_ready.sem, I.at(xc_ready, 1))
                        e.wait_ge(delta_done.sem, I.at(delta_done, i + 1))
                        e.tensor_tensor(out=rows_of(du[0:P, tile, :]), in0=rows_of(d),
                                        in1=in_time(xc[0:P, tile, :], k), op=ALU.mult).then_inc(du_done.sem, 1)

                def step(g, k, nh, tile, n):
                    s = g * NB + n
                    if n == 0 and nh == 0:
                        e.wait_ge(du_done.sem, I.at(du_done, k * T + tile + 1))
                    if tile == 0:
                        e.wait_ge(bc_ready.sem, I.at(bc_ready, (k * NH + nh) * 2 * NB + 2 * n + 1))
                    e.wait_ge(scan_done.sem, I.at(scan_done, s - SLOTS + 1))
                    e.tensor_tensor(out=db[0:P, s % SLOTS, :], in0=du[0:P, tile, :], in1=bc[0:P, 0, n, :],
                                    op=ALU.mult).then_inc(mul1_done.sem, 1)

                scans(T, idle, delta_of, idle, step, idle)

            images(e, lambda l: None, image)

        @block.scalar
        def _(e):
            e.sem_inc(y_evac.sem, 1)
            e.wait_ge(consts.sem, 9)
            e.activation(ln_one[:, :], one[:, :], ACT.Ln).then_inc(consts.sem, 1)

            def layer_start(l):
                weights_there(e, l)
                cl = l is None
                P, n, at = (PC, CT * K * NS, U_AL) if cl else (128, 3 * K * NS, V_AL)
                base = DEPTH * 2 if cl else l * 2
                e.activation(A[0:P, 0:n], vc[0:P, at:at + n], ACT.Exp).then_inc(w_made.sem, 1)
                e.wait_ge(w_made.sem, base + 1)
                e.activation(A[0:P, 0:n], A[0:P, 0:n], ACT.Copy, scale=-1.0).then_inc(w_made.sem, 1)
                e.wait_ge(w_made.sem, base + 2)

            def root(I, r):
                e.wait_ge(stats.sem, I.at(stats, 8 * (r + 1)))
                e.activation(sd[:, :], mv[:, :, 1], ACT.Sqrt, bias=eps[:, 0:1]).then_inc(sd_done.sem, 1)

            def turned_norm(I, n_turned, g_at, b_at, count):
                e.wait_ge(turned.sem, I.at(turned, n_turned))
                for c in range(CT):
                    ins = e.activation(xnT[:, c, :], bank2(2 * c, PC), ACT.Identity,
                                       scale=vc96[:, g_at + c:g_at + c + 1], bias=vc96[:, b_at + c:b_at + c + 1])
                ins.then_inc(turned_out.sem, 1)

            def image(I, b):
                P, T = I.P, I.T
                if I.closing:
                    e.wait_ge(turned.sem, I.at(turned, 1))
                    for c in range(CT):
                        ins = e.activation(xc[0:PC, c, :], bank2(2 * c, PC), ACT.Copy)
                    ins.then_inc(xc_ready.sem, 1)
                    e.wait_ge(xc_ready.sem, I.at(xc_ready, 1))
                else:
                    root(I, 0)
                    turned_norm(I, 1, 0, 2, 1)
                    for m in range(6):
                        e.wait_ge(in_proj.sem, I.at(in_proj, m + 1))
                        src = bank2(Y if m % 2 else ST)
                        if m < 3:
                            if m == 0:
                                e.wait_ge(pad_zero.sem, I.at(pad_zero, 1))
                            e.activation(xpad[:, m, 1:HH + 1, 1:WW + 1], src.rearrange("p (h w) -> p h w", h=HH),
                                         ACT.Copy).then_inc(in_evac.sem, 1)
                        else:
                            e.activation(zb[:, m - 3, :], src, ACT.Silu).then_inc(in_evac.sem, 1)
                    e.wait_ge(conv_step.sem, I.at(conv_step, 27))
                    for c in range(3):
                        ins = e.activation(xc[:, c, :], xc[:, c, :], ACT.Silu, bias=vc[:, V_CB + c:V_CB + c + 1])
                    ins.then_inc(xc_ready.sem, 1)
                    e.wait_ge(z_stored.sem, I.at(z_stored, 16))
                    e.wait_ge(xc_ready.sem, I.at(xc_ready, 1))

                def rows(k, stage):
                    if stage == 0:
                        e.wait_ge(st_full.sem, I.at(st_full, I.unit[("rows", k)] + 1))
                        e.wait_ge(lo_done.sem, I.at(lo_done, k))
                        e.activation(bcr[0:32, :], bank2(ST, 32), ACT.Copy)
                        e.activation(split[0:32, :], bank2(ST, 32), ACT.Copy).then_inc(hi_done.sem, 1)
                        e.activation(dts[:, :], ps[32:32 + R, ST:ST + 2, :].rearrange("p a b -> p (a b)"),
                                     ACT.Copy).then_inc(st_free.sem, 1)
                    if stage == 2:
                        e.wait_ge(r1_done.sem, I.at(r1_done, k + 1))
                        e.activation(split[32:64, :], bcr[32:64, :], ACT.Copy).then_inc(mid_done.sem, 1)

                def delta_of(k, tile, stage):
                    i = k * T + tile
                    if stage == 0:
                        bias = vc[0:P, I.dtb + i:I.dtb + i + 1]
                        e.wait_ge(st_full.sem, I.at(st_full, I.unit[("delta", k, tile)] + 1))
                        e.wait_ge(delta_done.sem, I.at(delta_done, i))
                        e.wait_ge(du_done.sem, I.at(du_done, max(i - T + 1, 0)))
                        if k >= 1:
                            e.wait_ge(exp_done.sem, I.at(exp_done, (((k - 1) * NH + 1) * T + tile + 1) * NB))
                        e.activation(sp_e[0:P, :], bank2(ST, P), ACT.Abs, bias=bias).then_inc(abs_done.sem, 1)
                        e.activation(delta[0:P, tile, :], bank2(ST, P), ACT.Relu, bias=bias)\
                            .then_inc(st_free.sem, 1)
                        e.wait_ge(abs_done.sem, I.at(abs_done, i + 1))
                        e.activation(sp_e[0:P, :], sp_e[0:P, :], ACT.Exp, scale=-1.0).then_inc(e_done.sem, 1)
                    if stage == 1:
                        e.wait_ge(e_done.sem, I.at(e_done, i + 1))
                        e.activation(sp_s[0:P, :], sp_e[0:P, :], ACT.Identity, bias=one[0:P, 0:1])\
                            .then_inc(s_done.sem, 1)
                        e.wait_ge(s_done.sem, I.at(s_done, i + 1))
                        e.activation(sp_l[0:P, :], sp_s[0:P, :], ACT.Ln).then_inc(ln_done.sem, 1)

                def spread(k, nh, i):
                    blk, n, w = k * NH + nh, i // 2, i % 2
                    e.wait_ge(st_full.sem, I.at(st_full, I.unit[("spread", k, nh, i)] + 1))
                    used = 0 if blk == 0 else (blk * T - 1) * NB + n + 1
                    reader = mul2_done if w else mul1_done
                    e.wait_ge(reader.sem, I.at(reader, used))
                    e.activation(bc[0:P, w, n, :], bank2(ST, P), ACT.Copy).then_inc(bc_ready.sem, 1)

                def step(g, k, nh, tile, n):
                    s = g * NB + n
                    if n == 0 and nh == 0:
                        e.wait_ge(delta_done.sem, I.at(delta_done, k * T + tile + 1))
                    col = (tile * K + k) * NS + nh * NB + n
                    e.wait_ge(mul2_done.sem, I.at(mul2_done, s - 1))
                    e.activation(bank2(2 * (s % 2), P), delta[0:P, tile, :], ACT.Exp,
                                 scale=A[0:P, col:col + 1]).then_inc(exp_done.sem, 1)

                def evac(g, k, nh, tile):
                    if (k, nh) != (K - 1, NH - 1):
                        e.wait_ge(summed.sem, I.at(summed, (g + 1) * NB))
                        e.activation(ysb[0:P, tile, :], bank2(Y, P), ACT.Copy).then_inc(y_evac.sem, 1)

                scans(T, rows, delta_of, spread, step, evac)

                if I.closing:
                    root(I, 0)
                    return
                root(I, 1)
                e.wait_ge(turned.sem, I.at(turned, 3))
                for c in range(3):
                    e.activation(gt[:, c, :], bank2(2 * c), ACT.Identity, scale=vc[:, V_OG + c:V_OG + c + 1],
                                 bias=vc[:, V_OB + c:V_OB + c + 1]).then_inc(scaled.sem, 1)
                root(I, 2)
                turned_norm(I, 4, 4, 6, 2)
                for m in range(MT):
                    e.wait_ge(up_proj.sem, I.at(up_proj, m + 1))
                    e.activation(hid[:, m, :], bank2(2 * (m % 4)), ACT.Gelu, bias=vc[:, V_B1 + m:V_B1 + m + 1])\
                        .then_inc(gelu_done.sem, 1)

            images(e, layer_start, image)

        @block.vector
        def _(e):
            e.sem_inc(scan_done.sem, SLOTS)
            e.sem_inc(mul2_done.sem, 2)
            e.sem_inc(lo_done.sem, 1)
            e.sem_inc(y_final.sem, 1)
            e.wait_ge(consts.sem, 10)

            def layer_start(l):
                weights_there(e, l)
                P, T, at = (PC, CT, U_DS) if l is None else (128, 3, V_DS)
                e.reduce_sum(ds_sum[0:P, 0:T], vc[0:P, at:at + T * K].rearrange("p (t k) -> p t k", k=K), axis=AX)\
                    .then_inc(ds_made.sem, 1)
                e.wait_ge(ds_made.sem, DEPTH + 1 if l is None else l + 1)
                e.sem_inc(gate_dve.sem, 1)

            def norm(I, r, src, dst, given, n_given):
                e.wait_ge(given.sem, I.at(given, n_given))
                for j in range(TOK):
                    e.bn_stats(st6[:, j, :], src(j)).then_inc(stats6.sem, 1)
                e.wait_ge(stats6.sem, I.at(stats6, 8 * r + 8))
                e.sem_inc(gate_dve.sem, 1)
                for j in range(TOK):
                    e.bn_aggr(mv[:, j, :], st6[:, j, :]).then_inc(stats.sem, 1)
                e.wait_ge(sd_done.sem, I.at(sd_done, r + 1))
                e.reciprocal(rstd[:, :], sd[:, :]).then_inc(rstd_done.sem, 1)
                e.wait_ge(rstd_done.sem, I.at(rstd_done, r + 1))
                for j in range(TOK):
                    ins = e.tensor_scalar(dst(j), src(j), mv[:, j, 0:1], rstd[:, j:j + 1],
                                          ALU.subtract, ALU.mult)
                ins.then_inc(normed.sem, 1)

            def image(I, b):
                P, T = I.P, I.T
                if not I.closing:
                    norm(I, 0, lambda j: xt[:, j, :], lambda j: xn[:, j, :], x_loaded, 16)
                    for tap in range(9):
                        dy, dx = tap // 3, tap % 3
                        for c in range(3):
                            if tap == 0:
                                e.wait_ge(in_evac.sem, I.at(in_evac, c + 1))
                            w = vc[:, V_CW + c * 9 + tap:V_CW + c * 9 + tap + 1]
                            win_ = xpad[:, c, dy:dy + HH, dx:dx + WW]
                            o_ = xc[:, c, :].rearrange("p (h w) -> p h w", h=HH)
                            if tap == 0:
                                e.tensor_scalar(o_, win_, w, None, ALU.mult).then_inc(conv_step.sem, 1)
                            else:
                                e.wait_ge(conv_step.sem, I.at(conv_step, (tap - 1) * 3 + c + 1))
                                e.scalar_tensor_tensor(out=o_, in0=win_, scalar=w, in1=o_, op0=ALU.mult,
                                                       op1=ALU.add).then_inc(conv_step.sem, 1)

                def rows(k, stage):
                    if stage == 1:
                        e.wait_ge(hi_done.sem, I.at(hi_done, k + 1))
                        e.tensor_tensor(out=bcr[32:64, :], in0=bcr[0:32, :], in1=split[0:32, :],
                                        op=ALU.subtract).then_inc(r1_done.sem, 1)
                    if stage == 3:
                        e.wait_ge(mid_done.sem, I.at(mid_done, k + 1))
                        e.tensor_tensor(out=split[64:96, :], in0=bcr[32:64, :], in1=split[32:64, :],
                                        op=ALU.subtract).then_inc(lo_done.sem, 1)

                def delta_of(k, tile, stage):
                    i, d = k * T + tile, delta[0:P, tile, :]
                    if stage == 2:
                        e.wait_ge(s_done.sem, I.at(s_done, i + 1))
                        e.scalar_tensor_tensor(out=sp_e[0:P, :], in0=sp_s[0:P, :], scalar=-1.0,
                                               in1=sp_e[0:P, :], op0=ALU.add, op1=ALU.subtract)\
                            .then_inc(rem_done.sem, 1)
                        e.wait_ge(ln_done.sem, I.at(ln_done, i + 1))
                        e.scalar_tensor_tensor(out=sp_l[0:P, :], in0=sp_l[0:P, :], scalar=ln_one[0:P, 0:1],
                                               in1=d, op0=ALU.subtract, op1=ALU.add).then_inc(sum_done.sem, 1)

                def step(g, k, nh, tile, n):
                    s = g * NB + n
                    a, b_ = bank2(2 * (s % 2), P), db[0:P, s % SLOTS, :]
                    e.wait_ge(exp_done.sem, I.at(exp_done, s + 1))
                    e.wait_ge(mul1_done.sem, I.at(mul1_done, s + 1))
                    e.tensor_tensor_scan(backward(a, k), backward(a, k), backward(b_, k), 0.0,
                                         ALU.mult, ALU.add).then_inc(scan_done.sem, 1)
                    if tile == 0:
                        e.wait_ge(bc_ready.sem, I.at(bc_ready, (k * NH + nh) * 2 * NB + 2 * n + 2))
                    e.wait_ge(summed.sem, I.at(summed, s - SLOTS + 1))
                    e.wait_ge(scan_done.sem, I.at(scan_done, s + 1))
                    e.tensor_tensor(out=hc[0:P, s % SLOTS, :], in0=a, in1=bc[0:P, 1, n, :], op=ALU.mult)\
                        .then_inc(mul2_done.sem, 1)

                def evac(g, k, nh, tile):
                    if (k, nh) == (K - 1, NH - 1):
                        e.wait_ge(summed.sem, I.at(summed, (g + 1) * NB))
                        e.scalar_tensor_tensor(out=ysb[0:P, tile, :], in0=xc[0:P, tile, :],
                                               scalar=ds_sum[0:P, tile:tile + 1], in1=bank2(Y, P),
                                               op0=ALU.mult, op1=ALU.add).then_inc(y_final.sem, 1)

                scans(T, rows, delta_of, idle, step, evac)

                if I.closing:
                    norm(I, 0, lambda j: ps[:, j, 0:C], lambda j: xt[:, j, :], turned, 2)
                    e.wait_ge(normed.sem, I.at(normed, 1))
                    e.tensor_tensor(out=xn, in0=xt, in1=lnw[:, 0:C].unsqueeze(1).broadcast_to((128, TOK, C)),
                                    op=ALU.mult).then_inc(x_new.sem, 1)
                    e.wait_ge(x_new.sem, I.at(x_new, 1))
                    e.tensor_tensor(out=xn, in0=xn, in1=lnw[:, C:2 * C].unsqueeze(1).broadcast_to((128, TOK, C)),
                                    op=ALU.add).then_inc(x_new.sem, 1)
                    return
                norm(I, 1, lambda j: ps[:, j, 0:DI], lambda j: yn[:, j, :], turned, 2)
                e.wait_ge(z_loaded.sem, I.at(z_loaded, 16))
                for c in range(3):
                    e.wait_ge(scaled.sem, I.at(scaled, c + 1))
                    ins = e.tensor_tensor(out=gt[:, c, :], in0=gt[:, c, :], in1=zb[:, c, :], op=ALU.mult)
                ins.then_inc(gated.sem, 1)
                e.wait_ge(out_proj.sem, I.at(out_proj, 1))
                e.wait_ge(x_loaded.sem, I.at(x_loaded, 32))
                e.tensor_tensor(out=xt, in0=ps[:, :, 0:C], in1=xt, op=ALU.add).then_inc(x_mid.sem, 1)
                norm(I, 2, lambda j: xt[:, j, :], lambda j: xn[:, j, :], x_mid, 1)
                e.wait_ge(down_proj.sem, I.at(down_proj, 1))
                e.tensor_tensor(out=xt, in0=ps[:, :, 0:C], in1=xt, op=ALU.add).then_inc(x_new.sem, 1)

            images(e, layer_start, image)

        @block.tensor
        def _(e):
            e.sem_inc(summed.sem, SLOTS)
            e.wait_ge(consts.sem, 9)

            def turn_tokens(src):
                for j in range(TOK):
                    for c in range(CT):
                        ins = e.transpose(ps[0:PC, 2 * c + j // 4, 128 * (j % 4):128 * (j % 4) + 128],
                                          src[:, j, PC * c:PC * c + PC], ident[:, :])
                ins.then_inc(turned.sem, 1)

            def image(I, b):
                P, T = I.P, I.T
                if I.closing:
                    e.wait_ge(x_loaded.sem, I.at(x_loaded, 16))
                    turn_tokens(xt)
                    e.wait_ge(xc_ready.sem, I.at(xc_ready, 1))
                else:
                    e.wait_ge(normed.sem, I.at(normed, 1))
                    turn_tokens(xn)
                    e.wait_ge(turned_out.sem, I.at(turned_out, 1))
                    for m in range(6):
                        if m >= 2:
                            e.wait_ge(in_evac.sem, I.at(in_evac, m - 1))
                        for half in range(2):
                            for c in range(CT):
                                ins = e.matmul(ps[:, (Y if m % 2 else ST) + half, :],
                                               win[:, c, 128 * m:128 * m + 128],
                                               xnT[:, c, HALF * half:HALF * half + HALF],
                                               start=c == 0, stop=c == CT - 1)
                        ins.then_inc(in_proj.sem, 1)
                    e.wait_ge(in_evac.sem, I.at(in_evac, 6))
                    e.wait_ge(xc_ready.sem, I.at(xc_ready, 1))

                def rows(k, stage):
                    if stage:
                        return
                    if ("rows", k) in I.free:
                        who, count_ = I.free[("rows", k)]
                        e.wait_ge(who.sem, I.at(who, count_))
                    for half in range(2):
                        for tile in range(T):
                            u_ = in_time(xc[0:P, tile, :], k)[:, 16 * half:16 * half + 16, :]
                            ins = e.matmul(ps[0:XR, ST + half, :].rearrange("p (a b) -> p a b", a=16),
                                           wxp[0:P, tile, k, :], u_, start=tile == 0, stop=tile == T - 1)
                    ins.then_inc(st_full.sem, 1)

                def delta_of(k, tile, stage):
                    if stage:
                        return
                    who, count_ = I.free[("delta", k, tile)]
                    e.wait_ge(who.sem, I.at(who, count_))
                    for half in range(2):
                        ins = e.matmul(ps[0:P, ST + half, :], wdt[:, k, tile * P:tile * P + P],
                                       dts[:, HALF * half:HALF * half + HALF], start=True, stop=True)
                    ins.then_inc(st_full.sem, 1)

                def spread(k, nh, i):
                    if (nh, i) == (0, 0):
                        e.wait_ge(lo_done.sem, I.at(lo_done, k + 1))
                    who, count_ = I.free[("spread", k, nh, i)]
                    e.wait_ge(who.sem, I.at(who, count_))
                    row = (i % 2) * NS + nh * NB + i // 2
                    for half in range(2):
                        ins = e.matmul(ps[0:P, ST + half, :], sel[:, row:row + 1].broadcast_to((96, P)),
                                       split[:, HALF * half:HALF * half + HALF], start=True, stop=True)
                    ins.then_inc(st_full.sem, 1)

                def step(g, k, nh, tile, n):
                    s = g * NB + n
                    first_block = (k, nh) == (0, 0)
                    if n == 0:
                        who, count_ = y_taken(I, g)
                        e.wait_ge(who.sem, I.at(who, count_))
                        if not first_block:
                            for half in range(2):
                                e.matmul(ps[0:P, Y + half, :], ident[0:P, 0:P],
                                         ysb[0:P, tile, HALF * half:HALF * half + HALF], start=True, stop=False)
                    e.wait_ge(mul2_done.sem, I.at(mul2_done, s + 1))
                    for half in range(2):
                        h_ = in_time(hc[0:P, s % SLOTS, :], k)[:, 16 * half:16 * half + 16, :]
                        ins = e.matmul(ps[0:P, Y + half, :].rearrange("p (a b) -> p a b", a=16),
                                       ident[0:P, 0:P], h_, start=first_block and n == 0, stop=n == NB - 1)
                    ins.then_inc(summed.sem, 1)

                scans(T, rows, delta_of, spread, step, idle, ahead=2)

                e.wait_ge(y_final.sem, I.at(y_final, T))
                for j in range(TOK):
                    for tile in range(T):
                        ins = e.transpose(ps[:, j, P * tile:P * tile + P], ysb[0:P, tile, 128 * j:128 * j + 128],
                                          ident[0:P, 0:P])
                ins.then_inc(turned.sem, 1)
                if I.closing:
                    return
                e.wait_ge(normed.sem, I.at(normed, 2))
                for tile in range(3):
                    for j in range(TOK):
                        ins = e.transpose(ps[:, 2 * tile + j // 4, 128 * (j % 4):128 * (j % 4) + 128],
                                          yn[:, j, 128 * tile:128 * tile + 128], ident[:, :])
                ins.then_inc(turned.sem, 1)
                e.wait_ge(gated.sem, I.at(gated, 1))
                for j in range(TOK):
                    for c in range(3):
                        ins = e.matmul(ps[:, j, 0:C], gt[:, c, 128 * j:128 * j + 128], wout[:, c, :],
                                       start=c == 0, stop=c == 2)
                ins.then_inc(out_proj.sem, 1)
                e.wait_ge(normed.sem, I.at(normed, 3))
                turn_tokens(xn)
                e.wait_ge(turned_out.sem, I.at(turned_out, 2))
                for m in range(MT):
                    if m >= 4:
                        e.wait_ge(gelu_done.sem, I.at(gelu_done, m - 3))
                    for half in range(2):
                        for c in range(CT):
                            ins = e.matmul(ps[:, 2 * (m % 4) + half, :], w1[:, c, 128 * m:128 * m + 128],
                                           xnT[:, c, HALF * half:HALF * half + HALF], start=c == 0, stop=c == CT - 1)
                    ins.then_inc(up_proj.sem, 1)
                e.wait_ge(gelu_done.sem, I.at(gelu_done, MT))
                for j in range(TOK):
                    for m in range(MT):
                        e.matmul(ps[:, j, 0:C], hid[:, m, 128 * j:128 * j + 128], w2[:, m, :],
                                 start=m == 0, stop=False)
                    ins = e.matmul(ps[:, j, 0:C], ones[:, :], b2r[:, :], start=False, stop=True)
                ins.then_inc(down_proj.sem, 1)

            def layer_start(l):
                weights_there(e, l)
                e.sem_inc(gate_pe.sem, 1)

            images(e, layer_start, image)


def kernel(**inputs):
    import numpy as np
    import concourse.bacc as bacc
    from concourse.bass_utils import run_bass_kernel_spmd as run

    g = {n: np.asarray(a) for n, a in inputs.items()}

    def by_partition(a, p):
        d, n = a.shape[:2]
        return np.moveaxis(a.reshape((d, n // p, p) + a.shape[2:]), 2, 1).reshape(d, p, -1)

    def xproj(a, p):
        a = np.concatenate([a[:, :, R:], a[:, :, :R]], axis=2)
        return by_partition(np.transpose(a, (0, 3, 1, 2)), p)

    def per_direction(a, p):
        return by_partition(np.swapaxes(a, 1, 2), p)

    def bias_cols(a, p):
        d, k, n = a.shape
        return np.transpose(a.reshape(d, k, n // p, p), (0, 3, 1, 2)).reshape(d, p, -1)

    P0 = "L0_conv_"
    v0 = np.concatenate([
        by_partition(g[P0 + "conv_w"].reshape(DEPTH, DI, 9), 128), by_partition(g[P0 + "conv_b"], 128),
        bias_cols(g[P0 + "dt_b"], 128), per_direction(g[P0 + "A_logs"], 128), per_direction(g[P0 + "Ds"], 128),
        by_partition(g[P0 + "ong"], 128), by_partition(g[P0 + "onb"], 128), by_partition(g[P0 + "b1"], 128)], axis=2)
    v96 = np.concatenate([by_partition(g[P0 + n], PC) for n in ("n1g", "n1b", "n2g", "n2b")], axis=2)
    P1 = "L1_conv_"
    v1 = np.concatenate([
        bias_cols(g[P1 + "dt_projs_bias"][None], PC), per_direction(g[P1 + "A_logs"].reshape(1, K, C, NS), PC),
        per_direction(g[P1 + "Ds"].reshape(1, K, C), PC)], axis=2)[0]
    named = {
        "x": g["x"],
        "w_in": by_partition(g[P0 + "in_w"], PC),
        "w_xp": xproj(g[P0 + "xproj_w"], 128),
        "w_dt": np.transpose(g[P0 + "dt_w"], (0, 3, 1, 2)).reshape(DEPTH, R, -1),
        "w_out": by_partition(g[P0 + "out_w"], 128),
        "w_1": by_partition(g[P0 + "w1"], PC),
        "w_2": by_partition(g[P0 + "w2"], 128),
        "vec": v0, "vec96": v96, "b2": g[P0 + "b2"].reshape(DEPTH, 1, C),
        "l_xp": xproj(g[P1 + "x_proj_weight"][None], PC)[0],
        "l_dt": np.transpose(g[P1 + "dt_projs_weight"], (2, 0, 1)).reshape(R, -1),
        "l_vec": v1,
        "l_ln": np.concatenate([g[P1 + "ln_weight"], g[P1 + "ln_bias"]]).reshape(1, -1),
    }
    nc = bacc.Bacc("TRN2", target_bir_lowering=False, num_devices=1)
    arrays, args = {}, []
    for name, a in named.items():
        a = np.ascontiguousarray(a)
        arrays[name + "_in"] = a
        args.append(nc.dram_tensor(name + "_in", a.shape, mybir.dt.from_np(a.dtype), kind="ExternalInput").ap())
    args.append(nc.dram_tensor("out_dram", (BATCH, HH, WW, C), mybir.dt.float32, kind="ExternalOutput").ap())
    build(nc, *args)
    r = run(nc, [arrays], core_ids=[0])
    return r.results[0]["out_dram"]
```

```python
import concourse.bass as bass
from concourse import mybir
from contextlib import ExitStack

BATCH, HH, WW, C = 4, 32, 32, 192
L = HH * WW
DEPTH, DI, NS, R, K, MLP = 9, 384, 16, 12, 4, 768
HALF = 512
TOK = L // 128
PC, CT = 96, 2
NB = 8
NH = NS // NB
EARLY = NB + 1
MT = MLP // 128
SLOTS = 4
XR = 2 * NS + R
LN_EPS = 1e-5

V_CW, V_CB, V_DTB, V_AL, V_DS, V_OG, V_OB, V_B1, V_END = 0, 27, 30, 42, 234, 246, 249, 252, 258
U_DTB, U_AL, U_DS, U_END = 0, 8, 136, 144


class Count:

    def __init__(self, sem, first, per0, per1):
        self.sem, self.first, self.per0, self.per1 = sem, first, per0, per1


def build(nc, x, w_in, w_xp, w_dt, w_out, w_1, w_2, vec, vec96, b2, l_xp, l_dt, l_vec, l_ln, out):
    f32, bf16 = mybir.dt.float32, mybir.dt.bfloat16
    ALU = mybir.AluOpType
    ACT = mybir.ActivationFunctionType
    AX = mybir.AxisListType.X

    ctx = ExitStack()
    with ctx:
        def sb(name, shape, dt=f32):
            return ctx.enter_context(nc.sbuf_tensor(name, shape, dt))

        x_dram = nc.dram_tensor("x_between", (2 * BATCH, L, C), f32, kind="Internal").ap()
        z_dram = nc.dram_tensor("z_parked", (128, 3 * L), f32, kind="Internal").ap()

        bc = sb("bc", [128, 2, NB, L])
        delta = sb("delta", [128, 3, L])
        du = sb("du", [128, 3, L])
        db = sb("db", [128, SLOTS, L])
        hc = sb("hc", [128, SLOTS, L])
        sp_e = sb("sp_e", [128, L])
        sp_s = sb("sp_s", [128, L])
        sp_l = sb("sp_l", [128, L])
        xc = sb("xc", [128, 3, L])
        ysb = sb("ysb", [128, 3, L])
        x_next = sb("x_next", [128, TOK, C])
        bcr = sb("bcr", [64, L])
        dts = sb("dts", [R, L])
        split = sb("split", [96, 2, L], bf16)
        sel = sb("sel", [96, 32], bf16)
        ident = sb("ident", [128, 128])
        ones = sb("ones", [1, 128])
        A = sb("A", [128, 3 * K * NS])
        ds_sum = sb("ds_sum", [128, 3])
        eps = sb("eps", [128, 1])
        one = sb("one", [128, 1])
        ln_one = sb("ln_one", [128, 1])
        win = sb("win", [PC, CT, 2 * DI])
        wxp = sb("wxp", [128, 3, K, XR])
        wdt = sb("wdt", [R, K, DI])
        wout = sb("wout", [128, 3, C])
        w1 = sb("w1", [PC, CT, MLP])
        w2 = sb("w2", [128, MT, C])
        vc = sb("vc", [128, V_END])
        vc96 = sb("vc96", [PC, 8])
        b2r = sb("b2r", [1, C])
        lnw = sb("lnw", [128, 2 * C])
        st6 = sb("st6", [128, TOK, 6])
        mv = sb("mv", [128, TOK, 2])
        sd = sb("sd", [128, TOK])
        rstd = sb("rstd", [128, TOK])

        flat = bc[:, :, :, :].rearrange("p a n l -> p (a n l)")
        o = 0

        def part(n, p=128):
            nonlocal o
            o += n
            return flat[0:p, o - n:o]
        xt = part(TOK * C).rearrange("p (j c) -> p j c", j=TOK)
        xn = part(TOK * C).rearrange("p (j c) -> p j c", j=TOK)
        xnT = part(CT * L, PC).rearrange("p (c t) -> p c t", c=CT)
        zb = part(3 * L).rearrange("p (c t) -> p c t", c=3)
        gt = part(3 * L).rearrange("p (c t) -> p c t", c=3)
        yn = part(TOK * DI).rearrange("p (j c) -> p j c", j=TOK)
        PAD = (HH + 2) * (WW + 2)
        xpad = flat[:, o - TOK * DI - 3 * L:o - TOK * DI - 3 * L + 3 * PAD].rearrange(
            "p (c h w) -> p c h w", c=3, h=HH + 2)
        hid = flat[:, o - TOK * DI - 3 * L:o - TOK * DI - 3 * L + MT * L].rearrange("p (m t) -> p m t", m=MT)
        assert o <= 2 * NB * L

        ps = ctx.enter_context(nc.psum_tensor("ps", [128, 8, HALF], f32))

        def bank2(b, p=128):
            return ps[0:p, b:b + 2, :].rearrange("p a b -> p (a b)")
        Y, ST = 4, 6

        def staging(k, nh, i):
            return (ST, 0, 2)[i % 3] if (k, nh) == (0, 0) and i < EARLY else ST


        def count(name, first=0, per0=0, per1=0):
            return Count(ctx.enter_context(nc.semaphore(name)), first, per0, per1)

        S0, S1 = K * NS * 3, K * NS * CT
        G0, G1 = K * NH * 3, K * NH * CT
        consts = count("consts")
        w_loaded = count("w_loaded")
        w_made = count("w_made")
        gate_pe = count("gate_pe")
        gate_dve = count("gate_dve")
        gate_act = count("gate_act")
        gate_sp = count("gate_sp")
        gate_pool = count("gate_pool")
        ds_made = count("ds_made")
        x_loaded = count("x_loaded", 0, 16, 16)
        next_loaded = count("next_loaded", 16, 16, 0)
        stats = count("stats", 8, 24, 8)
        stats6 = count("stats6", 8, 24, 8)
        sd_done = count("sd_done", 1, 3, 1)
        rstd_done = count("rstd_done", 1, 3, 1)
        normed = count("normed", 8, 24, 8)
        turned = count("turned", 0, 11, 9)
        turned_out = count("turned_out", 0, 2, 0)
        pad_zero = count("pad_zero", 0, 1, 0)
        in_proj = count("in_proj", 0, 6, 0)
        in_evac = count("in_evac", 0, 6, 0)
        conv_step = count("conv_step", 0, 27, 0)
        xc_ready = count("xc_ready", 0, 3, CT)
        z_stored = count("z_stored", 0, 16, 0)
        z_loaded = count("z_loaded", 0, 16, 0)
        st_full = count("st_full", 0, K * (1 + 3 + 2 * NS), K * (1 + CT + 2 * NS))
        st_free = count("st_free", 0, K * (1 + 3), K * (1 + CT))
        hi_done = count("hi_done", 0, K, K)
        r1_done = count("r1_done", 0, K, K)
        mid_done = count("mid_done", 0, K, K)
        lo_done = count("lo_done", 1, K, K)
        abs_done = count("abs_done", 0, K * 3, K * CT)
        e_done = count("e_done", 0, K * 3, K * CT)
        s_done = count("s_done", 0, K * 3, K * CT)
        ln_done = count("ln_done", 0, K * 3, K * CT)
        rem_done = count("rem_done", 0, K * 3, K * CT)
        sum_done = count("sum_done", 0, K * 3, K * CT)
        delta_done = count("delta_done", 1, K * 3, K * CT)
        du_done = count("du_done", 0, K * 3, K * CT)
        bc_ready = count("bc_ready", 0, K * 2 * NS, K * 2 * NS)
        exp_done = count("exp_done", 0, S0, S1)
        mul1_done = count("mul1_done", 2, S0, S1)
        scan_done = count("scan_done", SLOTS, S0, S1)
        mul2_done = count("mul2_done", 2, S0, S1)
        summed = count("summed", SLOTS, S0, S1)
        y_evac = count("y_evac", 1, G0 - 3, G1 - CT)
        y_final = count("y_final", 1, 3, CT)
        yT_out = count("yT_out", 0, 1, 0)
        scaled = count("scaled", 0, 3, 0)
        gated = count("gated", 0, 1, 0)
        out_proj = count("out_proj", 0, 8, 0)
        x_mid = count("x_mid", 0, 8, 0)
        up_proj = count("up_proj", 0, MT, 0)
        gelu_done = count("gelu_done", 0, MT, 0)
        down_proj = count("down_proj", 1, 8, 0)
        x_new = count("x_new", 1, 8, 2)
        x_stored = count("x_stored", 16, 32, 16)
        NW0, NW1 = 9, 4

        class Image:

            def __init__(self, closing, it):
                self.closing, self.it = closing, it
                self.P, self.T = (PC, CT) if closing else (128, 3)
                self.unit, self.free = UNITS[self.T]
                self.dtb = U_DTB if closing else V_DTB

            def at(self, c, k):
                if self.closing:
                    return self.it * c.per1 + (c.first + DEPTH * BATCH * c.per0 + k)
                return self.it * c.per0 + (c.first + k)

        SPREAD_3 = ((0,), (1,), (2,), (3,), (4,), (5,), (6,), ())
        SPREAD_2 = ((), (0,), (1,), (2, 3), (4,), (5, 6), (), ())

        def planned(*items):
            plan = {}
            for what, at in items:
                for p, *stages in at:
                    plan.setdefault(p, []).append((*what, stages))
            return plan

        LAST = ((("delta", 2), ((31, 0), (32, 1), (33, 2), (34, 3), (35, 4), (39, 5))),
                (("next rows",), ((35, 0), (36, 1), (37, 2), (38, 3), (39, 4), (40, 5), (41, 6))))
        PLAN_3 = planned((("delta", 0), ((9, 0), (10, 1), (11, 2), (12, 3), (13, 4), (17, 5))),
                         (("delta", 1), ((20, 0), (21, 1), (22, 2), (23, 3), (24, 4), (28, 5))), *LAST)
        FIRST_3 = planned((("delta", 1), ((24, 0), (25, 1), (26, 2, 3), (27, 4), (31, 5))), *LAST)
        PLAN_2 = planned((("rows",), ((6, 0, 1, 3, 4), (7, 5, 6))),
                         (("delta", 0), ((8, 0, 1), (9, 2, 3), (11, 4), (15, 5))),
                         (("delta", 1), ((16, 0, 1), (17, 2, 3), (19, 4), (23, 5))))

        def side_work(T, s):
            g, n = s // NB, s % NB
            k, nh, tile = g // (NH * T), g // T % NH, g % T
            nk, nn = (k, 1) if nh == 0 else (k + 1, 0)
            d, p = divmod(s + NB * T, NH * NB * T)
            found = []
            if tile == 0:
                at_n = (SPREAD_3 if T == 3 else SPREAD_2)[n]
                found += [("spread", k, nh, EARLY + i) for i in at_n]
            early = []
            if tile == T - 1 and nk < K:
                early = [("spread", nk, nn, n)] + [("spread", nk, nn, EARLY - 1)] * (n == NB - 1)
            if T == 3:
                found += early
            plan = (FIRST_3 if d == 0 else PLAN_3) if T == 3 else PLAN_2
            for what, *rest, stages in plan.get(p, ()):
                if what == "next rows" and d + 1 < K:
                    found += [("rows", d + 1, stage) for stage in stages]
                elif what != "next rows" and d < K:
                    found += [(what, d, *rest, stage) for stage in stages]
            return found if T == 3 else found + early

        def scans(T, rows, delta_of, spread, step, evac, ahead=0):
            do = {"rows": rows, "delta": delta_of, "spread": spread}
            for stage in [*range(T), 3, 4, 5, 6]:
                rows(0, stage)
            for stage in range(6):
                delta_of(0, 0, stage)
            for i in range(EARLY):
                spread(0, 0, i)
            steps = K * NS * T
            for s in range(ahead):
                for what, *args in side_work(T, s):
                    do[what](*args)
            for s in range(steps):
                g, n = s // NB, s % NB
                if ahead and s + ahead < steps:
                    for what, *args in side_work(T, s + ahead):
                        do[what](*args)
                step(g, g // (NH * T), g // T % NH, g % T, n)
                if not ahead:
                    for what, *args in side_work(T, s):
                        do[what](*args)
                if n == 1 and g:
                    h = g - 1
                    evac(h, h // (NH * T), h // T % NH, h % T)
            evac(g, K - 1, NH - 1, T - 1)

        def count_units(T):
            number, free, counts = {}, {}, {st_free: 0, bc_ready: 0}

            def unit(name, reader, banks=ST):
                if banks in before:
                    free[name] = before[banks]
                number[name] = len(number)
                counts[reader] += 1
                before[banks] = (reader, counts[reader])

            before = {}
            scans(T, lambda k, stage: stage or unit(("rows", k), st_free),
                  lambda k, tile, stage: stage or unit(("delta", k, tile), st_free),
                  lambda k, nh, i: unit(("spread", k, nh, i), bc_ready, staging(k, nh, i)), lambda *a: None, lambda *a: None)
            return number, free

        UNITS = {3: count_units(3), CT: count_units(CT)}

        def images(e, layer_start, image):
            with e.Fori(0, DEPTH) as l:
                layer_start(l)
                with e.Fori(0, BATCH) as b:
                    image(Image(False, l * BATCH + b), b)
            layer_start(None)
            with e.Fori(0, BATCH) as b:
                image(Image(True, b), b)

        def weights_there(e, l):
            e.wait_ge(w_loaded.sem, 16 * NW0 * DEPTH + 16 * NW1 if l is None else l * (16 * NW0) + 16 * NW0)

        def in_time(ap, k):
            return ap.rearrange("p (h w) -> p w h", h=HH) if k % 2 else ap.rearrange("p (h w) -> p h w", h=HH)

        def idle(*_):
            pass

        def rows_of(ap):
            return ap.rearrange("p (a b) -> p a b", a=32)

        def backward(ap, k):
            return ap[:, ::-1] if k >= 2 else ap

        def y_taken(I, g):
            n_act = (K * NH - 1) * I.T
            return (y_final, 0) if g == 0 else (y_evac, g) if g <= n_act else (y_final, g - n_act)

        block = ctx.enter_context(nc.Block())

        @block.sync
        def _(e):
            e.dma_start(x_dram[0:BATCH, :, :].rearrange("b t c -> (b t) c"), x.rearrange("b h w c -> (b h w) c"))\
                .then_inc(x_stored.sem, 16)
            e.dma_start(x_next[:, :, :], x[0:1, :, :, :].rearrange("o h w c -> (o h w) c")
                        .rearrange("(j p) c -> p j c", p=128)).then_inc(next_loaded.sem, 16)

            def layer_start(l):
                if l is None:
                    e.wait_ge(x_stored.sem, 16 + 32 * DEPTH * BATCH)
                    e.sem_inc(gate_sp.sem, 1)
                    for dst, src in ((wxp[0:PC, 0:CT, :, :].rearrange("p a b c -> p (a b c)"), l_xp),
                                     (wdt[:, :, 0:C], l_dt.rearrange("r (k d) -> r k d", k=K)),
                                     (vc[0:PC, 0:U_END], l_vec),
                                     (lnw[:, :], l_ln.broadcast_to((128, 2 * C)))):
                        e.dma_start(dst, src).then_inc(w_loaded.sem, 16)
                    return
                e.wait_ge(x_stored.sem, l * (32 * BATCH) + 16)
                e.sem_inc(gate_sp.sem, 1)
                for dst, src in ((win[:, :, :].rearrange("p a b -> p (a b)"), w_in),
                                 (wxp[:, :, :, :].rearrange("p a b c -> p (a b c)"), w_xp),
                                 (wdt[:, :, :].rearrange("p a b -> p (a b)"), w_dt),
                                 (wout[:, :, :].rearrange("p a b -> p (a b)"), w_out),
                                 (w1[:, :, :].rearrange("p a b -> p (a b)"), w_1),
                                 (w2[:, :, :].rearrange("p a b -> p (a b)"), w_2),
                                 (vc[:, :], vec), (vc96[:, :], vec96), (b2r[:, :], b2)):
                    e.dma_start(dst, src[bass.ds(l, 1), :, :].rearrange("o p n -> (o p) n"))\
                        .then_inc(w_loaded.sem, 16)

            def image(I, b):
                x_img = x_dram[bass.ds(b, 1), :, :].rearrange("o (j p) c -> p (o j) c", p=128)
                e.wait_ge(x_stored.sem, I.at(x_stored, 0))
                e.sem_inc(gate_sp.sem, 1)
                if I.closing:
                    e.dma_start(xt, x_img).then_inc(x_loaded.sem, 16)
                    e.wait_ge(x_new.sem, I.at(x_new, 2))
                    e.sem_inc(gate_sp.sem, 1)
                    e.dma_start(out[bass.ds(b, 1), :, :, :].rearrange("o h w c -> (o h w) c")
                                .rearrange("(j p) c -> p j c", p=128), xn).then_inc(x_stored.sem, 16)
                    return
                e.wait_ge(turned.sem, I.at(turned, 1))
                e.sem_inc(gate_sp.sem, 1)
                e.dma_start(x_next[:, :, :], x_dram[bass.ds(b + 1, 1), :, :].rearrange("o (j p) c -> p (o j) c", p=128))\
                    .then_inc(next_loaded.sem, 16)
                e.wait_ge(in_evac.sem, I.at(in_evac, 6))
                e.sem_inc(gate_sp.sem, 1)
                e.dma_start(z_dram.rearrange("p (c t) -> p c t", c=3), zb).then_inc(z_stored.sem, 16)
                e.wait_ge(z_stored.sem, I.at(z_stored, 16))
                e.sem_inc(gate_sp.sem, 1)
                e.wait_ge(summed.sem, I.at(summed, S0))
                e.sem_inc(gate_sp.sem, 1)
                e.wait_ge(mul1_done.sem, I.at(mul1_done, S0))
                e.sem_inc(gate_sp.sem, 1)
                e.dma_start(xt, x_img).then_inc(x_loaded.sem, 16)
                e.dma_start(zb, z_dram.rearrange("p (c t) -> p c t", c=3)).then_inc(z_loaded.sem, 16)
                e.wait_ge(x_new.sem, I.at(x_new, 8))
                e.sem_inc(gate_sp.sem, 1)
                e.dma_start(x_img, xt).then_inc(x_stored.sem, 16)
                e.dma_start(x_dram[bass.ds(b + BATCH, 1), :, :].rearrange("o (j p) c -> p (o j) c", p=128), xt)\
                    .then_inc(x_stored.sem, 16)

            images(e, layer_start, image)
            e.wait_ge(x_stored.sem, 16 + 32 * DEPTH * BATCH + 16 * BATCH)

        @block.gpsimd
        def _(e):
            e.sem_inc(mul1_done.sem, 2)
            e.sem_inc(delta_done.sem, 1)
            e.memset(ident[:, :], 0.0).then_inc(consts.sem, 1)
            e.memset(sel[:, :], 0.0).then_inc(consts.sem, 1)
            e.memset(ones[:, :], 1.0).then_inc(consts.sem, 1)
            e.memset(eps[:, :], LN_EPS).then_inc(consts.sem, 1)
            e.memset(one[:, :], 1.0).then_inc(consts.sem, 1)
            e.wait_ge(consts.sem, 2)
            e.affine_select(out=ident[:, :], in_=ident[:, :], compare_op=ALU.not_equal, fill=1.0, base=0,
                            pattern=[[-1, 128]], channel_multiplier=1).then_inc(consts.sem, 1)
            for third in range(3):
                e.wait_ge(consts.sem, 6 + third)
                e.affine_select(out=sel[:, :], in_=sel[:, :], compare_op=ALU.not_equal, fill=1.0,
                                base=-32 * third, pattern=[[-1, 32]], channel_multiplier=1)\
                    .then_inc(consts.sem, 1)

            def image(I, b):
                P, T = I.P, I.T
                if not I.closing:
                    e.wait_ge(down_proj.sem, I.at(down_proj, 0))
                    e.sem_inc(gate_pool.sem, 1)
                    e.memset(xpad, 0.0).then_inc(pad_zero.sem, 1)

                def delta_of(k, tile, stage):
                    i, d = k * T + tile, delta[0:P, tile, :]
                    if stage == 5:
                        e.wait_ge(rem_done.sem, I.at(rem_done, i + 1))
                        e.wait_ge(sum_done.sem, I.at(sum_done, i + 1))
                        e.tensor_tensor(out=d, in0=sp_l[0:P, :], in1=sp_e[0:P, :], op=ALU.subtract)\
                            .then_inc(delta_done.sem, 1)
                        if i == 0:
                            e.wait_ge(xc_ready.sem, I.at(xc_ready, T))
                        e.wait_ge(delta_done.sem, I.at(delta_done, i + 1))
                        e.tensor_tensor(out=rows_of(du[0:P, tile, :]), in0=rows_of(d),
                                        in1=in_time(xc[0:P, tile, :], k), op=ALU.mult).then_inc(du_done.sem, 1)

                def step(g, k, nh, tile, n):
                    s = g * NB + n
                    if n == 0 and nh == 0:
                        e.wait_ge(du_done.sem, I.at(du_done, k * T + tile + 1))
                    if tile == 0:
                        e.wait_ge(bc_ready.sem, I.at(bc_ready, (k * NH + nh) * 2 * NB + 2 * n + 1))
                    e.wait_ge(scan_done.sem, I.at(scan_done, s - SLOTS + 1))
                    e.tensor_tensor(out=db[0:P, s % SLOTS, :], in0=du[0:P, tile, :], in1=bc[0:P, 0, n, :],
                                    op=ALU.mult).then_inc(mul1_done.sem, 1)

                scans(T, idle, delta_of, idle, step, idle)

            images(e, lambda l: None, image)

        @block.scalar
        def _(e):
            e.sem_inc(y_evac.sem, 1)
            e.wait_ge(consts.sem, 9)
            e.preload_act_table_set("natural_log_exp_and_others")
            e.activation(ln_one[:, :], one[:, :], ACT.Ln).then_inc(consts.sem, 1)

            def layer_start(l):
                weights_there(e, l)
                cl = l is None
                P, n, at = (PC, CT * K * NS, U_AL) if cl else (128, 3 * K * NS, V_AL)
                base = DEPTH * 2 if cl else l * 2
                e.activation(A[0:P, 0:n], vc[0:P, at:at + n], ACT.Exp).then_inc(w_made.sem, 1)
                e.wait_ge(w_made.sem, base + 1)
                e.activation(A[0:P, 0:n], A[0:P, 0:n], ACT.Copy, scale=-1.0).then_inc(w_made.sem, 1)
                e.wait_ge(w_made.sem, base + 2)

            def root(I, r):
                e.wait_ge(stats.sem, I.at(stats, 8 * (r + 1)))
                e.activation(sd[:, :], mv[:, :, 1], ACT.Sqrt, bias=eps[:, 0:1]).then_inc(sd_done.sem, 1)

            e.wait_ge(stats.sem, TOK)
            e.activation(sd[:, :], mv[:, :, 1], ACT.Sqrt, bias=eps[:, 0:1]).then_inc(sd_done.sem, 1)

            def turned_norm(I, n_turned, g_at, b_at):
                e.wait_ge(turned.sem, I.at(turned, n_turned))
                for c in range(CT):
                    ins = e.activation(xnT[:, c, :], bank2(2 * c, PC), ACT.Identity,
                                       scale=vc96[:, g_at + c:g_at + c + 1], bias=vc96[:, b_at + c:b_at + c + 1])
                ins.then_inc(turned_out.sem, 1)

            def image(I, b):
                P, T = I.P, I.T
                if I.closing:
                    e.wait_ge(turned.sem, I.at(turned, 1))
                    for c in range(CT):
                        e.activation(xc[0:PC, c, :], bank2(2 * c, PC), ACT.Copy).then_inc(xc_ready.sem, 1)
                    e.wait_ge(xc_ready.sem, I.at(xc_ready, CT))
                else:
                    turned_norm(I, 1, 0, 2)
                    for m in range(6):
                        e.wait_ge(in_proj.sem, I.at(in_proj, m + 1))
                        src = bank2(Y if m % 2 else ST)
                        if m < 3:
                            if m == 0:
                                e.wait_ge(pad_zero.sem, I.at(pad_zero, 1))
                            e.activation(xpad[:, m, 1:HH + 1, 1:WW + 1], src.rearrange("p (h w) -> p h w", h=HH),
                                         ACT.Copy).then_inc(in_evac.sem, 1)
                        else:
                            e.activation(zb[:, m - 3, :], src, ACT.Silu).then_inc(in_evac.sem, 1)
                    for c in range(3):
                        e.wait_ge(conv_step.sem, I.at(conv_step, 25 + c))
                        e.activation(xc[:, c, :], xc[:, c, :], ACT.Silu, bias=vc[:, V_CB + c:V_CB + c + 1])\
                            .then_inc(xc_ready.sem, 1)
                    e.wait_ge(z_stored.sem, I.at(z_stored, 16))
                    e.wait_ge(x_stored.sem, I.at(x_stored, 0))
                    e.wait_ge(xc_ready.sem, I.at(xc_ready, 3))

                e.sem_inc(gate_act.sem, 1)
                e.preload_act_table_set("natural_log_exp_and_others")

                def rows(k, stage):
                    if stage == 3:
                        e.wait_ge(st_full.sem, I.at(st_full, I.unit[("rows", k)] + 1))
                        e.wait_ge(lo_done.sem, I.at(lo_done, k))
                        e.activation(bcr[0:32, :], bank2(ST, 32), ACT.Copy)
                        e.activation(split[0:32, k % 2, :], bank2(ST, 32), ACT.Copy).then_inc(hi_done.sem, 1)
                    if stage == 4:
                        e.activation(dts[:, :], ps[32:32 + R, ST:ST + 2, :].rearrange("p a b -> p (a b)"),
                                     ACT.Copy).then_inc(st_free.sem, 1)
                    if stage == 5:
                        e.wait_ge(r1_done.sem, I.at(r1_done, k + 1))
                        e.activation(split[32:64, k % 2, :], bcr[32:64, :], ACT.Copy).then_inc(mid_done.sem, 1)

                def delta_of(k, tile, stage):
                    i = k * T + tile
                    if stage == 0:
                        bias = vc[0:P, I.dtb + i:I.dtb + i + 1]
                        e.wait_ge(st_full.sem, I.at(st_full, I.unit[("delta", k, tile)] + 1))
                        e.wait_ge(delta_done.sem, I.at(delta_done, i))
                        e.wait_ge(du_done.sem, I.at(du_done, max(i - T + 1, 0)))
                        if k >= 1:
                            e.wait_ge(exp_done.sem, I.at(exp_done, (((k - 1) * NH + 1) * T + tile + 1) * NB))
                        e.activation(sp_e[0:P, :], bank2(ST, P), ACT.Abs, bias=bias).then_inc(abs_done.sem, 1)
                        e.activation(delta[0:P, tile, :], bank2(ST, P), ACT.Relu, bias=bias)\
                            .then_inc(st_free.sem, 1)
                    if stage == 1:
                        e.wait_ge(abs_done.sem, I.at(abs_done, i + 1))
                        e.activation(sp_e[0:P, :], sp_e[0:P, :], ACT.Exp, scale=-1.0).then_inc(e_done.sem, 1)
                    if stage == 2:
                        e.wait_ge(e_done.sem, I.at(e_done, i + 1))
                        e.activation(sp_s[0:P, :], sp_e[0:P, :], ACT.Identity, bias=one[0:P, 0:1])\
                            .then_inc(s_done.sem, 1)
                    if stage == 3:
                        e.wait_ge(s_done.sem, I.at(s_done, i + 1))
                        e.activation(sp_l[0:P, :], sp_s[0:P, :], ACT.Ln).then_inc(ln_done.sem, 1)

                def spread(k, nh, i):
                    blk, n, w = k * NH + nh, i // 2, i % 2
                    e.wait_ge(st_full.sem, I.at(st_full, I.unit[("spread", k, nh, i)] + 1))
                    used = 0 if blk == 0 else (blk * T - 1) * NB + n + 1
                    reader = mul2_done if w else mul1_done
                    e.wait_ge(reader.sem, I.at(reader, used))
                    e.activation(bc[0:P, w, n, :], bank2(staging(k, nh, i), P), ACT.Copy).then_inc(bc_ready.sem, 1)

                def step(g, k, nh, tile, n):
                    s = g * NB + n
                    if n == 0 and nh == 0:
                        e.wait_ge(delta_done.sem, I.at(delta_done, k * T + tile + 1))
                    col = (tile * K + k) * NS + nh * NB + n
                    if s < 2:
                        e.wait_ge(bc_ready.sem, I.at(bc_ready, EARLY))
                    e.wait_ge(mul2_done.sem, I.at(mul2_done, s - 1))
                    e.activation(bank2(2 * (s % 2), P), delta[0:P, tile, :], ACT.Exp,
                                 scale=A[0:P, col:col + 1]).then_inc(exp_done.sem, 1)

                def evac(g, k, nh, tile):
                    if (k, nh) != (K - 1, NH - 1):
                        e.wait_ge(summed.sem, I.at(summed, (g + 1) * NB))
                        e.activation(ysb[0:P, tile, :], bank2(Y, P), ACT.Copy).then_inc(y_evac.sem, 1)

                scans(T, rows, delta_of, spread, step, evac)

                if I.closing:
                    root(I, 0)
                    return
                root(I, 0)
                e.wait_ge(turned.sem, I.at(turned, 10))
                for c in range(3):
                    e.activation(gt[:, c, :], bank2(2 * c), ACT.Identity, scale=vc[:, V_OG + c:V_OG + c + 1],
                                 bias=vc[:, V_OB + c:V_OB + c + 1]).then_inc(scaled.sem, 1)
                root(I, 1)
                turned_norm(I, 11, 4, 6)
                root(I, 2)
                for m in range(MT):
                    e.wait_ge(up_proj.sem, I.at(up_proj, m + 1))
                    e.activation(hid[:, m, :], bank2(2 * (m % 4)), ACT.Gelu, bias=vc[:, V_B1 + m:V_B1 + m + 1])\
                        .then_inc(gelu_done.sem, 1)

            images(e, layer_start, image)

        @block.vector
        def _(e):
            e.sem_inc(scan_done.sem, SLOTS)
            e.sem_inc(mul2_done.sem, 2)
            e.sem_inc(lo_done.sem, 1)
            e.sem_inc(y_final.sem, 1)
            e.sem_inc(x_new.sem, 1)
            e.wait_ge(consts.sem, 10)

            def layer_start(l):
                weights_there(e, l)
                P, T, at = (PC, CT, U_DS) if l is None else (128, 3, V_DS)
                e.reduce_sum(ds_sum[0:P, 0:T], vc[0:P, at:at + T * K].rearrange("p (t k) -> p t k", k=K), axis=AX)\
                    .then_inc(ds_made.sem, 1)
                e.wait_ge(ds_made.sem, DEPTH + 1 if l is None else l + 1)
                e.sem_inc(gate_dve.sem, 1)

            def norm(I, r, src, dst, given, counts, before=None):
                for j in range(TOK):
                    if before:
                        before(j)
                    e.wait_ge(given.sem, I.at(given, counts[j]))
                    e.bn_stats(st6[:, j, :], src(j)).then_inc(stats6.sem, 1)
                e.wait_ge(stats6.sem, I.at(stats6, 8 * r + 8))
                moments()
                e.wait_ge(sd_done.sem, I.at(sd_done, r + 1))
                e.reciprocal(rstd[:, :], sd[:, :]).then_inc(rstd_done.sem, 1)
                e.wait_ge(rstd_done.sem, I.at(rstd_done, r + 1))
                to_norm(src, dst)

            def moments():
                e.sem_inc(gate_dve.sem, 1)
                for j in range(TOK):
                    e.bn_aggr(mv[:, j, :], st6[:, j, :]).then_inc(stats.sem, 1)

            def to_norm(src, dst):
                for j in range(TOK):
                    e.tensor_scalar(dst(j), src(j), mv[:, j, 0:1], rstd[:, j:j + 1],
                                    ALU.subtract, ALU.mult).then_inc(normed.sem, 1)

            def next_tile(j):
                return x_next[:, j, :]

            e.wait_ge(next_loaded.sem, 16)
            for j in range(TOK):
                e.bn_stats(st6[:, j, :], next_tile(j)).then_inc(stats6.sem, 1)
            e.wait_ge(stats6.sem, TOK)
            moments()
            e.wait_ge(sd_done.sem, 1)
            e.reciprocal(rstd[:, :], sd[:, :]).then_inc(rstd_done.sem, 1)
            e.wait_ge(rstd_done.sem, 1)
            to_norm(next_tile, next_tile)

            def image(I, b):
                P, T = I.P, I.T
                if not I.closing:
                    for tap in range(9):
                        dy, dx = tap // 3, tap % 3
                        for c in range(3):
                            if tap == 0:
                                e.wait_ge(in_evac.sem, I.at(in_evac, c + 1))
                            w = vc[:, V_CW + c * 9 + tap:V_CW + c * 9 + tap + 1]
                            win_ = xpad[:, c, dy:dy + HH, dx:dx + WW]
                            o_ = xc[:, c, :].rearrange("p (h w) -> p h w", h=HH)
                            if tap == 0:
                                e.tensor_scalar(o_, win_, w, None, ALU.mult).then_inc(conv_step.sem, 1)
                            else:
                                e.wait_ge(conv_step.sem, I.at(conv_step, (tap - 1) * 3 + c + 1))
                                e.scalar_tensor_tensor(out=o_, in0=win_, scalar=w, in1=o_, op0=ALU.mult,
                                                       op1=ALU.add).then_inc(conv_step.sem, 1)

                def rows(k, stage):
                    if stage == 4:
                        e.wait_ge(hi_done.sem, I.at(hi_done, k + 1))
                        e.tensor_tensor(out=bcr[32:64, :], in0=bcr[0:32, :], in1=split[0:32, k % 2, :],
                                        op=ALU.subtract).then_inc(r1_done.sem, 1)
                    if stage == 6:
                        e.wait_ge(mid_done.sem, I.at(mid_done, k + 1))
                        e.tensor_tensor(out=split[64:96, k % 2, :], in0=bcr[32:64, :], in1=split[32:64, k % 2, :],
                                        op=ALU.subtract).then_inc(lo_done.sem, 1)

                def delta_of(k, tile, stage):
                    i, d = k * T + tile, delta[0:P, tile, :]
                    if stage == 4:
                        e.wait_ge(s_done.sem, I.at(s_done, i + 1))
                        e.scalar_tensor_tensor(out=sp_e[0:P, :], in0=sp_s[0:P, :], scalar=-1.0,
                                               in1=sp_e[0:P, :], op0=ALU.add, op1=ALU.subtract)\
                            .then_inc(rem_done.sem, 1)
                        e.wait_ge(ln_done.sem, I.at(ln_done, i + 1))
                        e.scalar_tensor_tensor(out=sp_l[0:P, :], in0=sp_l[0:P, :], scalar=ln_one[0:P, 0:1],
                                               in1=d, op0=ALU.subtract, op1=ALU.add).then_inc(sum_done.sem, 1)

                def step(g, k, nh, tile, n):
                    s = g * NB + n
                    a, b_ = bank2(2 * (s % 2), P), db[0:P, s % SLOTS, :]
                    e.wait_ge(exp_done.sem, I.at(exp_done, s + 1))
                    e.wait_ge(mul1_done.sem, I.at(mul1_done, s + 1))
                    e.tensor_tensor_scan(backward(a, k), backward(a, k), backward(b_, k), 0.0,
                                         ALU.mult, ALU.add).then_inc(scan_done.sem, 1)
                    if tile == 0:
                        e.wait_ge(bc_ready.sem, I.at(bc_ready, (k * NH + nh) * 2 * NB + 2 * n + 2))
                    e.wait_ge(summed.sem, I.at(summed, s - SLOTS + 1))
                    e.wait_ge(scan_done.sem, I.at(scan_done, s + 1))
                    e.tensor_tensor(out=hc[0:P, s % SLOTS, :], in0=a, in1=bc[0:P, 1, n, :], op=ALU.mult)\
                        .then_inc(mul2_done.sem, 1)

                def evac(g, k, nh, tile):
                    if (k, nh) == (K - 1, NH - 1):
                        e.wait_ge(summed.sem, I.at(summed, (g + 1) * NB))
                        e.scalar_tensor_tensor(out=ysb[0:P, tile, :], in0=xc[0:P, tile, :],
                                               scalar=ds_sum[0:P, tile:tile + 1], in1=bank2(Y, P),
                                               op0=ALU.mult, op1=ALU.add).then_inc(y_final.sem, 1)

                scans(T, rows, delta_of, idle, step, evac)

                if I.closing:
                    norm(I, 0, lambda j: ps[:, j, 0:C], lambda j: xt[:, j, :], turned, range(2, 2 + TOK))
                    e.wait_ge(normed.sem, I.at(normed, TOK))
                    e.tensor_tensor(out=xn, in0=xt, in1=lnw[:, 0:C].unsqueeze(1).broadcast_to((128, TOK, C)),
                                    op=ALU.mult).then_inc(x_new.sem, 1)
                    e.wait_ge(x_new.sem, I.at(x_new, 1))
                    e.tensor_tensor(out=xn, in0=xn, in1=lnw[:, C:2 * C].unsqueeze(1).broadcast_to((128, TOK, C)),
                                    op=ALU.add).then_inc(x_new.sem, 1)
                    return
                norm(I, 0, lambda j: ps[:, j, 0:DI], lambda j: yn[:, j, :], turned, range(2, 2 + TOK))
                e.wait_ge(z_loaded.sem, I.at(z_loaded, 16))
                for c in range(3):
                    e.wait_ge(scaled.sem, I.at(scaled, c + 1))
                    ins = e.tensor_tensor(out=gt[:, c, :], in0=gt[:, c, :], in1=zb[:, c, :], op=ALU.mult)
                ins.then_inc(gated.sem, 1)
                e.wait_ge(x_loaded.sem, I.at(x_loaded, 16))

                def add_y(j):
                    e.wait_ge(out_proj.sem, I.at(out_proj, j + 1))
                    e.tensor_tensor(out=xt[:, j, :], in0=ps[:, j, 0:C], in1=xt[:, j, :], op=ALU.add)\
                        .then_inc(x_mid.sem, 1)

                norm(I, 1, lambda j: xt[:, j, :], lambda j: xn[:, j, :], x_mid, range(1, 1 + TOK), before=add_y)
                norm(I, 2, next_tile, next_tile, next_loaded, [16] * TOK)
                for j in range(TOK):
                    e.wait_ge(down_proj.sem, I.at(down_proj, j + 1))
                    e.tensor_tensor(out=xt[:, j, :], in0=ps[:, j, 0:C], in1=xt[:, j, :], op=ALU.add)\
                        .then_inc(x_new.sem, 1)

            images(e, layer_start, image)

        @block.tensor
        def _(e):
            e.sem_inc(summed.sem, SLOTS)
            e.sem_inc(down_proj.sem, 1)
            e.wait_ge(consts.sem, 9)

            def turn_token_tile(src, j):
                for c in range(CT):
                    ins = e.transpose(ps[0:PC, 2 * c + j // 4, 128 * (j % 4):128 * (j % 4) + 128],
                                      src[:, j, PC * c:PC * c + PC], ident[:, :])
                return ins

            def turn_tokens(src):
                for j in range(TOK):
                    ins = turn_token_tile(src, j)
                ins.then_inc(turned.sem, 1)

            def image(I, b):
                P, T = I.P, I.T
                if I.closing:
                    e.wait_ge(x_loaded.sem, I.at(x_loaded, 16))
                    turn_tokens(xt)
                    e.wait_ge(xc_ready.sem, I.at(xc_ready, CT))
                else:
                    e.wait_ge(normed.sem, I.at(normed, 0))
                    e.wait_ge(x_new.sem, I.at(x_new, 0))
                    turn_tokens(x_next)
                    e.wait_ge(turned_out.sem, I.at(turned_out, 1))
                    for m in range(6):
                        if m >= 2:
                            e.wait_ge(in_evac.sem, I.at(in_evac, m - 1))
                        for half in range(2):
                            for c in range(CT):
                                ins = e.matmul(ps[:, (Y if m % 2 else ST) + half, :],
                                               win[:, c, 128 * m:128 * m + 128],
                                               xnT[:, c, HALF * half:HALF * half + HALF],
                                               start=c == 0, stop=c == CT - 1)
                        ins.then_inc(in_proj.sem, 1)
                    e.wait_ge(in_evac.sem, I.at(in_evac, 6))

                def rows(k, stage):
                    if stage >= T:
                        return
                    if stage == 0 and ("rows", k) in I.free:
                        who, count_ = I.free[("rows", k)]
                        e.wait_ge(who.sem, I.at(who, count_))
                    if k == 0:
                        e.wait_ge(xc_ready.sem, I.at(xc_ready, stage + 1))
                    for half in range(2):
                        u_ = in_time(xc[0:P, stage, :], k)[:, 16 * half:16 * half + 16, :]
                        ins = e.matmul(ps[0:XR, ST + half, :].rearrange("p (a b) -> p a b", a=16),
                                       wxp[0:P, stage, k, :], u_, start=stage == 0, stop=stage == T - 1)
                    if stage == T - 1:
                        ins.then_inc(st_full.sem, 1)

                def delta_of(k, tile, stage):
                    if stage:
                        return
                    who, count_ = I.free[("delta", k, tile)]
                    e.wait_ge(who.sem, I.at(who, count_))
                    for half in range(2):
                        ins = e.matmul(ps[0:P, ST + half, :], wdt[:, k, tile * P:tile * P + P],
                                       dts[:, HALF * half:HALF * half + HALF], start=True, stop=True)
                    ins.then_inc(st_full.sem, 1)

                def spread(k, nh, i):
                    if (nh, i) == (0, 0):
                        e.wait_ge(lo_done.sem, I.at(lo_done, k + 1))
                    if ("spread", k, nh, i) in I.free:
                        who, count_ = I.free[("spread", k, nh, i)]
                        e.wait_ge(who.sem, I.at(who, count_))
                    row = (i % 2) * NS + nh * NB + i // 2
                    for half in range(2):
                        ins = e.matmul(ps[0:P, staging(k, nh, i) + half, :], sel[:, row:row + 1].broadcast_to((96, P)),
                                       split[:, k % 2, HALF * half:HALF * half + HALF], start=True, stop=True)
                    ins.then_inc(st_full.sem, 1)

                def step(g, k, nh, tile, n):
                    s = g * NB + n
                    first_block = (k, nh) == (0, 0)
                    if n == 0:
                        who, count_ = y_taken(I, g)
                        e.wait_ge(who.sem, I.at(who, count_))
                        if not first_block:
                            for half in range(2):
                                e.matmul(ps[0:P, Y + half, :], ident[0:P, 0:P],
                                         ysb[0:P, tile, HALF * half:HALF * half + HALF], start=True, stop=False)
                    e.wait_ge(mul2_done.sem, I.at(mul2_done, s + 1))
                    for half in range(2):
                        h_ = in_time(hc[0:P, s % SLOTS, :], k)[:, 16 * half:16 * half + 16, :]
                        ins = e.matmul(ps[0:P, Y + half, :].rearrange("p (a b) -> p a b", a=16),
                                       ident[0:P, 0:P], h_, start=first_block and n == 0, stop=n == NB - 1)
                    ins.then_inc(summed.sem, 1)

                scans(T, rows, delta_of, spread, step, idle, ahead=2)

                e.wait_ge(y_final.sem, I.at(y_final, T))
                for j in range(TOK):
                    for tile in range(T):
                        ins = e.transpose(ps[:, j, P * tile:P * tile + P], ysb[0:P, tile, 128 * j:128 * j + 128],
                                          ident[0:P, 0:P])
                    ins.then_inc(turned.sem, 1)
                if I.closing:
                    return
                e.wait_ge(normed.sem, I.at(normed, TOK))
                for j in range(TOK):
                    for tile in range(3):
                        ins = e.transpose(ps[:, 2 * tile + j // 4, 128 * (j % 4):128 * (j % 4) + 128],
                                          yn[:, j, 128 * tile:128 * tile + 128], ident[:, :])
                ins.then_inc(turned.sem, 1)
                e.wait_ge(gated.sem, I.at(gated, 1))
                for j in range(TOK):
                    for c in range(3):
                        ins = e.matmul(ps[:, j, 0:C], gt[:, c, 128 * j:128 * j + 128], wout[:, c, :],
                                       start=c == 0, stop=c == 2)
                    ins.then_inc(out_proj.sem, 1)
                for j in range(TOK):
                    e.wait_ge(normed.sem, I.at(normed, TOK + j + 1))
                    ins = turn_token_tile(xn, j)
                ins.then_inc(turned.sem, 1)
                e.wait_ge(turned_out.sem, I.at(turned_out, 2))
                for m in range(MT):
                    if m >= 4:
                        e.wait_ge(gelu_done.sem, I.at(gelu_done, m - 3))
                    for half in range(2):
                        for c in range(CT):
                            ins = e.matmul(ps[:, 2 * (m % 4) + half, :], w1[:, c, 128 * m:128 * m + 128],
                                           xnT[:, c, HALF * half:HALF * half + HALF], start=c == 0, stop=c == CT - 1)
                    ins.then_inc(up_proj.sem, 1)
                e.wait_ge(gelu_done.sem, I.at(gelu_done, MT))
                for j in range(TOK):
                    for m in range(MT):
                        e.matmul(ps[:, j, 0:C], hid[:, m, 128 * j:128 * j + 128], w2[:, m, :],
                                 start=m == 0, stop=False)
                    e.matmul(ps[:, j, 0:C], ones[:, :], b2r[:, :], start=False, stop=True)\
                        .then_inc(down_proj.sem, 1)

            def layer_start(l):
                weights_there(e, l)
                e.sem_inc(gate_pe.sem, 1)

            images(e, layer_start, image)


def kernel(**inputs):
    import numpy as np
    import concourse.bacc as bacc
    from concourse.bass_utils import run_bass_kernel_spmd as run

    g = {n: np.asarray(a) for n, a in inputs.items()}

    def by_partition(a, p):
        d, n = a.shape[:2]
        return np.moveaxis(a.reshape((d, n // p, p) + a.shape[2:]), 2, 1).reshape(d, p, -1)

    def xproj(a, p):
        a = np.concatenate([a[:, :, R:], a[:, :, :R]], axis=2)
        return by_partition(np.transpose(a, (0, 3, 1, 2)), p)

    def per_direction(a, p):
        return by_partition(np.swapaxes(a, 1, 2), p)

    def bias_cols(a, p):
        d, k, n = a.shape
        return np.transpose(a.reshape(d, k, n // p, p), (0, 3, 1, 2)).reshape(d, p, -1)

    P0 = "L0_conv_"
    v0 = np.concatenate([
        by_partition(g[P0 + "conv_w"].reshape(DEPTH, DI, 9), 128), by_partition(g[P0 + "conv_b"], 128),
        bias_cols(g[P0 + "dt_b"], 128), per_direction(g[P0 + "A_logs"], 128), per_direction(g[P0 + "Ds"], 128),
        by_partition(g[P0 + "ong"], 128), by_partition(g[P0 + "onb"], 128), by_partition(g[P0 + "b1"], 128)], axis=2)
    v96 = np.concatenate([by_partition(g[P0 + n], PC) for n in ("n1g", "n1b", "n2g", "n2b")], axis=2)
    P1 = "L1_conv_"
    v1 = np.concatenate([
        bias_cols(g[P1 + "dt_projs_bias"][None], PC), per_direction(g[P1 + "A_logs"].reshape(1, K, C, NS), PC),
        per_direction(g[P1 + "Ds"].reshape(1, K, C), PC)], axis=2)[0]
    named = {
        "x": g["x"],
        "w_in": by_partition(g[P0 + "in_w"], PC),
        "w_xp": xproj(g[P0 + "xproj_w"], 128),
        "w_dt": np.transpose(g[P0 + "dt_w"], (0, 3, 1, 2)).reshape(DEPTH, R, -1),
        "w_out": by_partition(g[P0 + "out_w"], 128),
        "w_1": by_partition(g[P0 + "w1"], PC),
        "w_2": by_partition(g[P0 + "w2"], 128),
        "vec": v0, "vec96": v96, "b2": g[P0 + "b2"].reshape(DEPTH, 1, C),
        "l_xp": xproj(g[P1 + "x_proj_weight"][None], PC)[0],
        "l_dt": np.transpose(g[P1 + "dt_projs_weight"], (2, 0, 1)).reshape(R, -1),
        "l_vec": v1,
        "l_ln": np.concatenate([g[P1 + "ln_weight"], g[P1 + "ln_bias"]]).reshape(1, -1),
    }
    nc = bacc.Bacc("TRN2", target_bir_lowering=False, num_devices=1)
    arrays, args = {}, []
    for name, a in named.items():
        a = np.ascontiguousarray(a)
        arrays[name + "_in"] = a
        args.append(nc.dram_tensor(name + "_in", a.shape, mybir.dt.from_np(a.dtype), kind="ExternalInput").ap())
    args.append(nc.dram_tensor("out_dram", (BATCH, HH, WW, C), mybir.dt.float32, kind="ExternalOutput").ap())
    build(nc, *args)
    r = run(nc, [arrays], core_ids=[0])
    return r.results[0]["out_dram"]
```
